# Optimizing a Trainium2 kernel written in Bass

```python
import numpy as np
import jax
import jax.numpy as jnp

def _softmax(x, axis=-1):
    return jax.nn.softmax(x, axis=axis)

def _gelu(x):
    return jax.nn.gelu(x, approximate=True)

def _silu(x):
    return jax.nn.silu(x)

def _sigmoid(x):
    return jax.nn.sigmoid(x)

def _layernorm(x, axis=-1, eps=1e-05):
    m = jnp.mean(x, axis=axis, keepdims=True)
    v = jnp.var(x, axis=axis, keepdims=True)
    return (x - m) / jnp.sqrt(v + eps)

def _scatter_add(tgt, idx, src, axis=0):
    return tgt.at[idx].add(src)

def _segment_sum(src, seg, n):
    return jax.ops.segment_sum(src, seg, n)
kernel_name = 'mk_prb_d1_jaxref_r8_ec2a3d'

def setup_inputs(seed: int=0):
    np.random.seed(seed)
    _w = jnp.asarray

    def _L0_attn_setup():
        import jax, jax.numpy as jnp
        import numpy as np
        B, S, D = (2, 256, 128)
        H, DH = (16, 64)
        DQL, DKVL = (64, 64)
        DR = 64
        TOPK = 64
        LN_EPS = 1e-05
        ROPE_BASE = 10000.0

        def _rope_tables(seq_len, dim):
            inv_freq = 1.0 / ROPE_BASE ** (np.arange(0, dim, 2, dtype=np.float32) / dim)
            t = np.arange(seq_len, dtype=np.float32)
            freqs = np.outer(t, inv_freq)
            cos = np.concatenate([np.cos(freqs), np.cos(freqs)], -1)[:, ::2]
            sin = np.concatenate([np.sin(freqs), np.sin(freqs)], -1)[:, ::2]
            return (jnp.asarray(cos), jnp.asarray(sin))

        def _apply_rope_subspace(x, d_rope):
            s = x.shape[-2]
            cos, sin = _rope_tables(s, d_rope)
            xr, xp = (x[..., :d_rope], x[..., d_rope:])
            e, o = (xr[..., 0::2], xr[..., 1::2])
            rot = jnp.stack([e * cos - o * sin, e * sin + o * cos], axis=-1).reshape(xr.shape)
            return jnp.concatenate([rot, xp], axis=-1)

        def _reference_tuple_inner(x, w_down_q, w_down_kv, w_up_q, w_up_k, w_up_v, w_out, ln_scale, ln_bias):
            b, s, d = x.shape
            residual = x
            mu = jnp.mean(x, axis=-1, keepdims=True)
            var = jnp.mean((x - mu) ** 2, axis=-1, keepdims=True)
            h = (x - mu) * jax.lax.rsqrt(var + LN_EPS) * ln_scale + ln_bias
            c_q = h @ w_down_q.T
            c_kv = h @ w_down_kv.T
            q = (c_q @ w_up_q.T).reshape(b, s, H, DH).transpose(0, 2, 1, 3)
            k = (c_kv @ w_up_k.T).reshape(b, s, H, DH).transpose(0, 2, 1, 3)
            v = (c_kv @ w_up_v.T).reshape(b, s, H, DH).transpose(0, 2, 1, 3)
            q = _apply_rope_subspace(q, DR)
            k = _apply_rope_subspace(k, DR)
            scale = 1.0 / np.sqrt(DH).astype(np.float32)
            scores = jnp.einsum('bhqd,bhkd->bhqk', q, k) * scale
            _, indices = jax.lax.top_k(scores, min(TOPK, s))
            attn = jax.nn.softmax(scores, axis=-1)
            out = jnp.einsum('bhqk,bhkd->bhqd', attn, v)
            out = out.transpose(0, 2, 1, 3).reshape(b, s, H * DH)
            out = out @ w_out.T + residual
            return (out, indices.astype(jnp.int64))
        key = jax.random.key(seed)
        ks = jax.random.split(key, 7)
        init = lambda k, shape: jax.random.normal(k, shape, jnp.float32) * 0.02
        return {'x': jax.random.normal(ks[0], (B, S, D), jnp.float32), 'w_down_q': init(ks[1], (DQL, D)), 'w_down_kv': init(ks[2], (DKVL, D)), 'w_up_q': init(ks[3], (H * DH, DQL)), 'w_up_k': init(ks[4], (H * DH, DKVL)), 'w_up_v': init(ks[5], (H * DH, DKVL)), 'w_out': init(ks[6], (D, H * DH)), 'ln_scale': jnp.ones((D,), jnp.float32), 'ln_bias': jnp.zeros((D,), jnp.float32)}
    _L0_attn_in = _L0_attn_setup()

    def _L0_ffn_setup():
        import jax, jax.numpy as jnp
        import numpy as np
        import math
        BETA = 0.9
        THRESHOLD = 1.0
        NUM_STEPS = 5
        ALPHA = 2.0

        @jax.custom_vjp
        def spike_fn(u):
            return (u > 0).astype(u.dtype)

        def _spike_fwd(u):
            return (spike_fn(u), u)

        def _spike_bwd(u, g):
            s = jnp.pi / 2.0 * ALPHA * u
            return (g * (ALPHA / 2.0) / (1.0 + s * s),)
        spike_fn.defvjp(_spike_fwd, _spike_bwd)
        key = jax.random.key(seed)
        k1, k2, k3 = jax.random.split(key, 3)
        n_embd = 128
        x = jax.random.normal(k1, (4, 256, n_embd), dtype=jnp.float32)
        W_fc = jax.random.normal(k2, (4 * n_embd, n_embd), dtype=jnp.float32) / math.sqrt(n_embd)
        W_proj = jax.random.normal(k3, (n_embd, 4 * n_embd), dtype=jnp.float32) / math.sqrt(4 * n_embd)
        return {'x': x, 'W_fc': W_fc, 'W_proj': W_proj}
    _L0_ffn_in = _L0_ffn_setup()
    _d = {'L0_attn_x': _L0_attn_in['x'], 'L0_attn_w_down_q': _L0_attn_in['w_down_q'], 'L0_attn_w_down_kv': _L0_attn_in['w_down_kv'], 'L0_attn_w_up_q': _L0_attn_in['w_up_q'], 'L0_attn_w_up_k': _L0_attn_in['w_up_k'], 'L0_attn_w_up_v': _L0_attn_in['w_up_v'], 'L0_attn_w_out': _L0_attn_in['w_out'], 'L0_attn_ln_scale': _L0_attn_in['ln_scale'], 'L0_attn_ln_bias': _L0_attn_in['ln_bias'], 'L0_ffn_W_fc': _L0_ffn_in['W_fc'], 'L0_ffn_W_proj': _L0_ffn_in['W_proj']}
    _x0 = _d['L0_attn_x']
    _d['L0_attn_x'] = jax.random.normal(jax.random.fold_in(jax.random.key(seed), 1), (32, 256, 128), dtype=_x0.dtype)
    del _x0
    return _d

def reference(L0_attn_x, L0_attn_w_down_q, L0_attn_w_down_kv, L0_attn_w_up_q, L0_attn_w_up_k, L0_attn_w_up_v, L0_attn_w_out, L0_attn_ln_scale, L0_attn_ln_bias, L0_ffn_W_fc, L0_ffn_W_proj):

    def _L0_attn_ref(x, w_down_q, w_down_kv, w_up_q, w_up_k, w_up_v, w_out, ln_scale, ln_bias):
        import jax, jax.numpy as jnp
        import numpy as np
        B, S, D = (2, 256, 128)
        H, DH = (16, 64)
        DQL, DKVL = (64, 64)
        DR = 64
        TOPK = 64
        LN_EPS = 1e-05
        ROPE_BASE = 10000.0

        def _rope_tables(seq_len, dim):
            inv_freq = 1.0 / ROPE_BASE ** (np.arange(0, dim, 2, dtype=np.float32) / dim)
            t = np.arange(seq_len, dtype=np.float32)
            freqs = np.outer(t, inv_freq)
            cos = np.concatenate([np.cos(freqs), np.cos(freqs)], -1)[:, ::2]
            sin = np.concatenate([np.sin(freqs), np.sin(freqs)], -1)[:, ::2]
            return (jnp.asarray(cos), jnp.asarray(sin))

        def _apply_rope_subspace(x, d_rope):
            s = x.shape[-2]
            cos, sin = _rope_tables(s, d_rope)
            xr, xp = (x[..., :d_rope], x[..., d_rope:])
            e, o = (xr[..., 0::2], xr[..., 1::2])
            rot = jnp.stack([e * cos - o * sin, e * sin + o * cos], axis=-1).reshape(xr.shape)
            return jnp.concatenate([rot, xp], axis=-1)

        def _reference_tuple_inner(x, w_down_q, w_down_kv, w_up_q, w_up_k, w_up_v, w_out, ln_scale, ln_bias):
            b, s, d = x.shape
            residual = x
            mu = jnp.mean(x, axis=-1, keepdims=True)
            var = jnp.mean((x - mu) ** 2, axis=-1, keepdims=True)
            h = (x - mu) * jax.lax.rsqrt(var + LN_EPS) * ln_scale + ln_bias
            c_q = h @ w_down_q.T
            c_kv = h @ w_down_kv.T
            q = (c_q @ w_up_q.T).reshape(b, s, H, DH).transpose(0, 2, 1, 3)
            k = (c_kv @ w_up_k.T).reshape(b, s, H, DH).transpose(0, 2, 1, 3)
            v = (c_kv @ w_up_v.T).reshape(b, s, H, DH).transpose(0, 2, 1, 3)
            q = _apply_rope_subspace(q, DR)
            k = _apply_rope_subspace(k, DR)
            scale = 1.0 / np.sqrt(DH).astype(np.float32)
            scores = jnp.einsum('bhqd,bhkd->bhqk', q, k) * scale
            _, indices = jax.lax.top_k(scores, min(TOPK, s))
            attn = jax.nn.softmax(scores, axis=-1)
            out = jnp.einsum('bhqk,bhkd->bhqd', attn, v)
            out = out.transpose(0, 2, 1, 3).reshape(b, s, H * DH)
            out = out @ w_out.T + residual
            return (out, indices.astype(jnp.int64))
        return _reference_tuple_inner(x, w_down_q, w_down_kv, w_up_q, w_up_k, w_up_v, w_out, ln_scale, ln_bias)[0]

    def _L0_ffn_ref(x, W_fc, W_proj):
        import jax, jax.numpy as jnp
        import numpy as np
        import math
        BETA = 0.9
        THRESHOLD = 1.0
        NUM_STEPS = 5
        ALPHA = 2.0

        @jax.custom_vjp
        def spike_fn(u):
            return (u > 0).astype(u.dtype)

        def _spike_fwd(u):
            return (spike_fn(u), u)

        def _spike_bwd(u, g):
            s = jnp.pi / 2.0 * ALPHA * u
            return (g * (ALPHA / 2.0) / (1.0 + s * s),)
        spike_fn.defvjp(_spike_fwd, _spike_bwd)
        h = jnp.square(jax.nn.relu(jnp.einsum('bsd,fd->bsf', x, W_fc)))
        y = jnp.einsum('bsf,df->bsd', h, W_proj)

        def step(mem, _):
            reset = jax.lax.stop_gradient(spike_fn(mem - THRESHOLD))
            mem_new = BETA * mem + y - reset * THRESHOLD
            spk = spike_fn(mem_new - THRESHOLD)
            return (mem_new, spk)
        mem0 = jnp.zeros_like(y)
        _, spks = jax.lax.scan(step, mem0, None, length=NUM_STEPS)
        return jnp.sum(spks, axis=0) / NUM_STEPS
    x = L0_attn_x
    xn = _layernorm(x, axis=-1)
    x = x + _L0_attn_ref(xn, L0_attn_w_down_q, L0_attn_w_down_kv, L0_attn_w_up_q, L0_attn_w_up_k, L0_attn_w_up_v, L0_attn_w_out, L0_attn_ln_scale, L0_attn_ln_bias) + _L0_ffn_ref(xn, L0_ffn_W_fc, L0_ffn_W_proj)
    return x

_drawn_inputs = setup_inputs


def setup_inputs(seed=0):
    import zlib

    import numpy as np

    out = dict(_drawn_inputs(seed))
    spreads = {'L0_attn_ln_scale': (1.0, 0.6), 'L0_attn_ln_bias': (0.0, 0.8)}
    factors = {'L0_attn_w_down_q': 8.0,
     'L0_attn_w_down_kv': 8.0,
     'L0_attn_w_up_q': 8.0,
     'L0_attn_w_up_k': 8.0,
     'L0_attn_w_up_v': 8.0,
     'L0_attn_w_out': 8.0,
     'L0_ffn_W_fc': 2.687}
    for name, (base, spread) in spreads.items():
        noise = np.random.default_rng([zlib.crc32(name.encode()), seed]).standard_normal(out[name].shape)
        drawn = base * np.exp(spread * noise) if base else spread * noise
        out[name] = jnp.asarray(drawn.astype(out[name].dtype))
    for name, factor in factors.items():
        out[name] = (out[name] * factor).astype(out[name].dtype)
    return out
```

```python
from contextlib import ExitStack

import numpy as np

import concourse.bass as bass
from concourse import mybir

F32 = mybir.dt.float32
F32R = mybir.dt.float32r
ALU = mybir.AluOpType
ACT = mybir.ActivationFunctionType
AXIS_X = mybir.AxisListType.X

B, S, D = 32, 256, 128
H, DH, L = 16, 64, 64
F = 512
P = 128
TT = S // P
PAIRS = H // 2
STEPS = B * PAIRS
UNROLL = 2
BODY = UNROLL * PAIRS
FC = F // P
LN_EPS = 1e-5
BETA, THRESHOLD, NUM_STEPS = 0.9, 1.0, 5
HEAD = 2


def done(n):
    return n + 1 + HEAD


def beyond(n, end):
    return isinstance(n, int) and n >= end


def build(nc, x, wup, wdown2, wkv_t, wv, wo_t, ln_cols, wfc_t, wproj_t, rope, ident, out):
    ctx = ExitStack()
    with ctx:
        def sb(name, shape, dt=F32):
            return ctx.enter_context(nc.sbuf_tensor(name, shape, dt))

        def pb(name, shape):
            return ctx.enter_context(nc.psum_tensor(name, shape, F32))

        def sem(name):
            return ctx.enter_context(nc.semaphore(name))

        wup_raw = sb("wup_raw", [P, 4, H * DH])
        wup_hi = sb("wup_hi", [P, 4, H * DH], F32R)
        wup_lo = sb("wup_lo", [P, 4, H * DH], F32R)
        wdown_sb = sb("wdown_sb", [P, 2, 2 * L])
        wkv_sb = sb("wkv_sb", [P, L])
        wv_sb = sb("wv_sb", [P, PAIRS, L])
        wo_sb = sb("wo_sb", [P, PAIRS, D])
        wvo_sb = sb("wvo_sb", [P, PAIRS, D])
        ln_sb = sb("ln_sb", [P, 2])
        wfc_sb = sb("wfc_sb", [P, F])
        wproj_sb = sb("wproj_sb", [P, FC, D])
        rope_sb = sb("rope_sb", [P, 2, 2, S])
        ident_sb = sb("ident_sb", [P, P])
        minus_half = sb("minus_half", [P, TT])
        x_sb = sb("x_sb", [P, 2, TT, D])
        xn_sb = sb("xn_sb", [P, 2, TT, D])
        z_sb = sb("z_sb", [P, TT, D])
        stats = sb("stats", [P, 2, TT, 6])
        moments = sb("moments", [P, 2, TT, 2])
        var_eps = sb("var_eps", [P, 2, TT])
        rstd = sb("rstd", [P, 2, TT])
        h_t = sb("h_t", [P, S])
        xn_t = sb("xn_t", [P, S])
        latent = sb("latent", [P, 2, 2, S], F32R)
        ckv = sb("ckv", [P, 2, TT, L])
        relu_sb = sb("relu_sb", [P, FC, S])
        hidden = sb("hidden", [P, FC, S])
        neg_y = sb("neg_y", [P, 2, TT * D])
        mem_t = sb("mem_t", [P, TT * D])
        mem = sb("mem", [P, 2, TT * D])
        spikes = sb("spikes", [P, 2, TT * D])
        acc = sb("acc", [P, TT * D])
        out_sb = sb("out_sb", [P, 2, TT, D])
        rotated = sb("rotated", [P, 2, 2, 2, S])
        qk = sb("qk", [P, 2, 2, S])
        neg_max = sb("neg_max", [P, 2, 2, TT])
        den = sb("den", [P, 2, 2, TT])
        rden = sb("rden", [P, 2, 2, TT])
        prob = sb("prob", [P, 2, 2, TT, S])
        prob_t = sb("prob_t", [P, 2, 2, TT, S])
        u_t = sb("u_t", [P, PAIRS, S])
        ps_q = pb("ps_q", [P, 2, S])
        ps_k = pb("ps_k", [P, 2, S])
        ps_s = [pb(f"ps_s{h}", [P, TT, S]) for h in range(2)]
        ps_t = [pb(f"ps_t{h}", [P, TT, S]) for h in range(2)]
        ps_u = pb("ps_u", [P, 512])
        ps_m = pb("ps_m", [P, 512])

        w_loaded = sem("w_loaded")
        x_loaded = [sem(f"x_loaded{i}") for i in range(2)]
        stored = [sem(f"stored{i}") for i in range(2)]
        setup_dve = sem("setup_dve")
        setup_pool = sem("setup_pool")
        setup_pe = sem("setup_pe")
        dve_waited, pool_waited = sem("dve_waited"), sem("pool_waited")
        q_up, k_up = sem("q_up"), sem("k_up")
        q_rot, k_rot = sem("q_rot"), sem("k_rot")
        rope_done = sem("rope_done")
        s_ready = [sem(f"s_ready{h}") for h in range(2)]
        max_ready = [sem(f"max_ready{h}") for h in range(2)]
        exp_done = [sem(f"exp_done{h}") for h in range(2)]
        rden_ready = [sem(f"rden_ready{h}") for h in range(2)]
        p_norm = [sem(f"p_norm{h}") for h in range(2)]
        t_ready = [sem(f"t_ready{h}") for h in range(2)]
        pt_ready = [sem(f"pt_ready{h}") for h in range(2)]
        u_ready = sem("u_ready")
        u_evac = sem("u_evac")
        stats1, aggr1 = sem("stats1"), sem("aggr1")
        eps1, rstd1 = sem("eps1"), sem("rstd1")
        xn_ready = sem("xn_ready")
        stats2, aggr2 = sem("stats2"), sem("aggr2")
        eps2, rstd2 = sem("eps2"), sem("rstd2")
        z_ready = sem("z_ready")
        tr_ready, tr_evac = sem("tr_ready"), sem("tr_evac")
        cc_ready = sem("cc_ready")
        latent_hi, latent_split = sem("latent_hi"), sem("latent_split")
        ckv_mm, ckv_ready = sem("ckv_mm"), sem("ckv_ready")
        fc_ready, relu_done, sq_done = sem("fc_ready"), sem("relu_done"), sem("sq_done")
        y_ready, ny_ready = sem("y_ready"), sem("ny_ready")
        res_ready = sem("res_ready")
        lif = sem("lif")
        out_ready, final_done = sem("out_ready"), sem("final_done")
        LIF_OPS = 3 * NUM_STEPS - 1

        by_engine = {
            "pe": [q_up, k_up, *s_ready, *t_ready, u_ready, tr_ready, cc_ready, ckv_mm, fc_ready, y_ready,
                   out_ready],
            "dve": [q_rot, k_rot, *max_ready, *rden_ready, u_evac, stats1, aggr1, xn_ready, stats2, aggr2,
                    z_ready, latent_hi, latent_split, lif, final_done],
            "act": [*exp_done, *pt_ready, tr_evac, ckv_ready, relu_done, ny_ready],
            "pool": [rope_done, *p_norm, eps1, rstd1, eps2, rstd2, sq_done, res_ready],
        }

        def start_counters(eng, who):
            for s in by_engine[who]:
                eng.sem_inc(s, HEAD)

        loads = [
            (ln_sb[:, :], ln_cols), (ident_sb[:, :], ident),
            (wdown_sb[:, :, :], wdown2), (wkv_sb[:, :], wkv_t),
            (wup_raw[0:L, :, :], wup), (wup_raw[L:P, :, :], wup),
            (rope_sb[:, :, :, :], rope),
            (wv_sb[:, :, :], wv), (wo_sb[:, :, :], wo_t),
            (wfc_sb[:, :], wfc_t), (wproj_sb[:, :, :], wproj_t),
        ]
        W_ALL = 16 * len(loads)
        x_v = x.rearrange("b (t p) d -> b p t d", p=P)
        out_v = out.rearrange("b (t p) d -> b p t d", p=P)

        block = ctx.enter_context(nc.Block())

        def run(eng, prologue, body):
            prologue()
            with eng.Fori(0, B // UNROLL - 1) as i:
                body(i)
            body(B // UNROLL - 1)

        @block.sync
        def _(sp):
            def load_x(n, par):
                sp.dma_start(x_sb[:, par, :, :], x_v[n]).then_inc(x_loaded[par], 16)

            def prologue():
                load_x(0, 0)
                load_x(1, 1)
                for dst, src in loads:
                    sp.dma_start(dst, src).then_inc(w_loaded, 16)

            def body(i):
                for b0 in range(UNROLL):
                    b = i * UNROLL + b0
                    if not beyond(b + 2, B):
                        sp.wait_ge(res_ready, done(b))
                        load_x(b + 2, b0)
                    sp.wait_ge(final_done, done(b))
                    sp.dma_start(out_v[b], out_sb[:, b0, :, :]).then_inc(stored[b0], 16)

            run(sp, prologue, body)
            for par in range(2):
                sp.wait_ge(stored[par], 16 * (B // 2) + 16)

        @block.tensor
        def _(pe):
            def project(g, s, which):
                up, rot, bank = (q_up, q_rot, ps_q) if which == 0 else (k_up, k_rot, ps_k)
                if s % PAIRS == 0 and which == 0:
                    pe.wait_ge(latent_split, done(batch_of(g, s)))
                pe.wait_ge(rot, done(g - 1))
                pair, par = s % PAIRS, (s // PAIRS) % 2
                for j in range(2):
                    cols = slice(pair * P, (pair + 1) * P)
                    rhs = latent[:, par, which, :]
                    nc.tensor.matmul(bank[:, j, :], wup_hi[:, 2 * which + j, cols], rhs, start=True, stop=False)
                    last = nc.tensor.matmul(bank[:, j, :], wup_lo[:, 2 * which + j, cols], rhs,
                                            start=False, stop=True)
                last.then_inc(up, 1)

            def scores(g, s, h):
                if h == 0:
                    pe.wait_ge(rope_done, done(g))
                pe.wait_ge(exp_done[h], done(g - 1))
                rows = slice(h * DH, (h + 1) * DH)
                for t in range(TT):
                    last = nc.tensor.matmul(ps_s[h][:, t, :], qk[rows, s % 2, 0, t * P:(t + 1) * P],
                                            qk[rows, s % 2, 1, :], start=True, stop=True)
                last.then_inc(s_ready[h], 1)

            def transpose_probs(g, s, h):
                pe.wait_ge(p_norm[h], done(g))
                pe.wait_ge(pt_ready[h], done(g - 1))
                for kt in range(TT):
                    for t in range(TT):
                        last = nc.tensor.transpose(ps_t[h][:, kt, t * P:(t + 1) * P],
                                                   prob[:, s % 2, h, t, kt * P:(kt + 1) * P], ident_sb[:, :])
                last.then_inc(t_ready[h], 1)

            def weigh_latents(g, s):
                for h in range(2):
                    pe.wait_ge(pt_ready[h], done(g))
                pe.wait_ge(u_evac, done(g - 1))
                if s % PAIRS == 0:
                    pe.wait_ge(ckv_ready, done(batch_of(g, s)))
                for kt in range(TT):
                    for h in range(2):
                        last = nc.tensor.matmul(ps_u[h * L:(h + 1) * L, 0:S], ckv[:, (s // PAIRS) % 2, kt, :],
                                                prob_t[:, s % 2, h, kt, :], start=(kt == 0), stop=(kt == TT - 1))
                last.then_inc(u_ready, 1)

            def transpose_inputs(n, par):
                pe.wait_ge(z_ready, done(n))
                pe.wait_ge(final_done, done(n - 2))
                for src, at in ((z_sb[:, :, :], 0), (xn_sb[:, par, :, :], S)):
                    for t in range(TT):
                        last = nc.tensor.transpose(ps_m[:, at + t * P:at + (t + 1) * P], src[:, t, :], ident_sb[:, :])
                last.then_inc(tr_ready, 1)

            def latents(n):
                pe.wait_ge(tr_evac, done(n))
                for which in range(2):
                    last = nc.tensor.matmul(ps_m[:, which * S:(which + 1) * S], wdown_sb[:, which, :], h_t[:, :],
                                            start=True, stop=True)
                last.then_inc(cc_ready, 1)

            def latents_by_token(n):
                pe.wait_ge(latent_split, done(n))
                for t in range(TT):
                    last = nc.tensor.matmul(ps_m[:, t * L:(t + 1) * L], h_t[:, t * P:(t + 1) * P], wkv_sb[:, :],
                                            start=True, stop=True)
                last.then_inc(ckv_mm, 1)

            def ffn_in(n, half):
                if half == 0:
                    pe.wait_ge(ckv_ready, done(n))
                else:
                    pe.wait_ge(relu_done, done(2 * n))
                for j in range(2):
                    c = 2 * half + j
                    last = nc.tensor.matmul(ps_m[:, j * S:(j + 1) * S], wfc_sb[:, c * P:(c + 1) * P], xn_t[:, :],
                                            start=True, stop=True)
                last.then_inc(fc_ready, 1)

            def ffn_out(n):
                pe.wait_ge(sq_done, done(2 * n + 1))
                for t in range(TT):
                    for c in range(FC):
                        last = nc.tensor.matmul(ps_m[:, t * D:(t + 1) * D], hidden[:, c, t * P:(t + 1) * P],
                                                wproj_sb[:, c, :], start=(c == 0), stop=(c == FC - 1))
                last.then_inc(y_ready, 1)

            def attention_out(b, g):
                pe.wait_ge(u_evac, done(g))
                if not beyond(b + 1, B):
                    pe.wait_ge(ny_ready, done(b + 1))
                for t in range(TT):
                    for pair in range(PAIRS):
                        last = nc.tensor.matmul(ps_m[:, t * D:(t + 1) * D], u_t[:, pair, t * P:(t + 1) * P],
                                                wvo_sb[:, pair, :], start=(pair == 0), stop=(pair == PAIRS - 1))
                last.then_inc(out_ready, 1)

            def extras(b, g, b0, p):
                n, par = b + 1, (b0 + 1) % 2
                if p == PAIRS - 1:
                    attention_out(b, g)
                if beyond(n, B):
                    return
                if p == 0:
                    transpose_inputs(n, par)
                elif p == 1:
                    latents(n)
                elif p == 2:
                    latents_by_token(n)
                elif p in (3, 4):
                    ffn_in(n, p - 3)
                elif p == 6:
                    ffn_out(n)

            def prologue():
                start_counters(pe, "pe")
                pe.wait_ge(w_loaded, W_ALL)
                for half in range(2):
                    for j in range(PAIRS // 2):
                        pair = half * PAIRS // 2 + j
                        for h in range(2):
                            rows = slice(h * DH, (h + 1) * DH)
                            last = nc.tensor.matmul((ps_u if half == 0 else ps_q.rearrange("p a s -> p (a s)"))
                                                    [h * L:(h + 1) * L, j * D:(j + 1) * D],
                                                    wv_sb[rows, pair, :], wo_sb[rows, pair, :],
                                                    start=True, stop=True)
                last.then_inc(setup_pe, 1)
                pe.wait_ge(setup_dve, 2)
                transpose_inputs(0, 0)
                latents(0)
                latents_by_token(0)
                project(0, 0, 0)
                project(0, 0, 1)
                ffn_in(0, 0)
                ffn_in(0, 1)
                project(1, 1, 0)
                project(1, 1, 1)
                scores(0, 0, 0)
                scores(0, 0, 1)
                ffn_out(0)
                project(2, 2, 0)
                project(2, 2, 1)
                scores(1, 1, 0)
                transpose_probs(0, 0, 0)
                scores(1, 1, 1)
                transpose_probs(0, 0, 1)

            def body(i):
                for s in range(BODY):
                    g, b0, p = i * BODY + s, s // PAIRS, s % PAIRS
                    weigh_latents(g, s)
                    for h in range(2):
                        if not beyond(g + 2, STEPS):
                            scores(g + 2, s + 2, h)
                        if not beyond(g + 1, STEPS):
                            transpose_probs(g + 1, s + 1, h)
                        if not beyond(g + 3, STEPS):
                            project(g + 3, s + 3, h)
                        if h == 0:
                            extras(i * UNROLL + b0, g, b0, p)

            batch_base = {}

            def batch_of(g, s):
                return batch_base["i"] * UNROLL + s // PAIRS

            def with_base(f):
                def g(i):
                    batch_base["i"] = i
                    f(i)
                return g

            batch_base["i"] = 0
            run(pe, prologue, with_base(body))

        @block.scalar
        def _(act):
            def exponentials(g, s, h):
                act.wait_ge(max_ready[h], done(g))
                act.wait_ge(t_ready[h], done(g - 2))
                for t in range(TT):
                    last = nc.scalar.activation(prob[:, s % 2, h, t, :], ps_s[h][:, t, :], ACT.Exp,
                                                bias=neg_max[:, s % 2, h, t:t + 1],
                                                accum_out=den[:, s % 2, h, t:t + 1])
                last.then_inc(exp_done[h], 1)

            def copy_transposed(g, s, h):
                act.wait_ge(t_ready[h], done(g))
                act.wait_ge(u_ready, done(g - 2))
                nc.scalar.copy(prob_t[:, s % 2, h, :, :], ps_t[h][:, :, :]).then_inc(pt_ready[h], 1)

            def copy_inputs(n):
                act.wait_ge(tr_ready, done(n))
                act.wait_ge(w_loaded, W_ALL)
                nc.scalar.activation(h_t[:, :], ps_m[:, 0:S], ACT.Identity, bias=ln_sb[:, 1:2], scale=ln_sb[:, 0:1])
                nc.scalar.copy(xn_t[:, :], ps_m[:, S:2 * S]).then_inc(tr_evac, 1)

            def copy_latents(n, par):
                act.wait_ge(ckv_mm, done(n))
                nc.scalar.copy(ckv[:, par, :, :], ps_m[:, 0:TT * L].rearrange("p (t l) -> p t l", t=TT))\
                    .then_inc(ckv_ready, 1)

            def relu(n, half):
                act.wait_ge(fc_ready, done(2 * n + half))
                nc.scalar.activation(relu_sb[:, 2 * half:2 * half + 2, :],
                                     ps_m[:, :].rearrange("p (c s) -> p c s", c=2), ACT.Relu).then_inc(relu_done, 1)

            def negate_y(n, par):
                act.wait_ge(y_ready, done(n))
                nc.scalar.mul(neg_y[:, par, :], ps_m[:, 0:TT * D], -1.0).then_inc(ny_ready, 1)

            def prologue():
                start_counters(act, "act")
                copy_inputs(0)
                copy_latents(0, 0)
                relu(0, 0)
                relu(0, 1)
                exponentials(0, 0, 0)
                exponentials(0, 0, 1)
                negate_y(0, 0)
                exponentials(1, 1, 0)
                copy_transposed(0, 0, 0)
                exponentials(1, 1, 1)
                copy_transposed(0, 0, 1)

            def body(i):
                for s in range(BODY):
                    g, b0, p = i * BODY + s, s // PAIRS, s % PAIRS
                    n, par = i * UNROLL + b0 + 1, (b0 + 1) % 2
                    for h in range(2):
                        if not beyond(g + 2, STEPS):
                            exponentials(g + 2, s + 2, h)
                        if not beyond(g + 1, STEPS):
                            copy_transposed(g + 1, s + 1, h)
                        if h == 0 and not beyond(n, B):
                            if p == 0:
                                copy_inputs(n)
                            elif p == 2:
                                copy_latents(n, par)
                            elif p in (3, 4):
                                relu(n, p - 3)
                            elif p == 6:
                                negate_y(n, par)

            run(act, prologue, body)

        @block.vector
        def _(dve):
            def rotate(g, s, which):
                up, rot, bank = (q_up, q_rot, ps_q) if which == 0 else (k_up, k_rot, ps_k)
                dve.wait_ge(up, done(g))
                dve.wait_ge(rope_done, done(g - 2))
                nc.vector.tensor_tensor(rotated[:, s % 2, which, :, :], bank[:, :, :], rope_sb[:, which, :, :],
                                        ALU.mult).then_inc(rot, 1)

            def row_max(g, s, h):
                dve.wait_ge(s_ready[h], done(g))
                dve.wait_ge(exp_done[h], done(g - 2))
                nc.vector.tensor_reduce(neg_max[:, s % 2, h, :], ps_s[h][:, :, :], AXIS_X, ALU.max,
                                        negate=True).then_inc(max_ready[h], 1)

            def reciprocals(g, s, h):
                dve.wait_ge(exp_done[h], done(g))
                dve.wait_ge(p_norm[h], done(g - 2))
                nc.vector.reciprocal(rden[:, s % 2, h, :], den[:, s % 2, h, :]).then_inc(rden_ready[h], 1)

            def copy_u(g, s):
                dve.wait_ge(u_ready, done(g))
                if s % PAIRS == 0:
                    dve.wait_ge(out_ready, done(batch_base["i"] * UNROLL + s // PAIRS - 1))
                nc.vector.tensor_copy(u_t[:, s % PAIRS, :], ps_u[:, 0:S]).then_inc(u_evac, 1)

            def moments_of(n, par, which):
                src, st, ag = ((x_sb, stats1, aggr1), (xn_sb, stats2, aggr2))[which]
                if which == 0:
                    dve.wait_ge(x_loaded[par], 16 * (n // 2 if isinstance(n, int) else batch_base["i"] + 1) + 16)
                    dve.wait_ge(aggr1, done(n - 1))
                else:
                    dve.wait_ge(xn_ready, done(n))
                    dve.wait_ge(aggr2, done(n - 1))
                for t in range(TT):
                    last = nc.vector.bn_stats(stats[:, which, t, :], src[:, par, t, :])
                last.then_inc(st, 1)
                dve.wait_ge(st, done(n))
                dve.wait_ge((xn_ready, z_ready)[which], done(n - 1))
                dve.sem_inc(dve_waited, 1)
                for t in range(TT):
                    last = nc.vector.bn_aggr(moments[:, which, t, :], stats[:, which, t, :])
                last.then_inc(ag, 1)

            def normalise(n, par, which):
                if which == 0:
                    dve.wait_ge(rstd1, done(n))
                    dve.wait_ge(res_ready, done(n - 2))
                    dve.wait_ge(tr_ready, done(n - 2))
                    src, dst, ready = x_sb[:, par, :, :], xn_sb[:, par, :, :], xn_ready
                else:
                    dve.wait_ge(rstd2, done(n))
                    dve.wait_ge(tr_ready, done(n - 1))
                    src, dst, ready = xn_sb[:, par, :, :], z_sb[:, :, :], z_ready
                for t in range(TT):
                    last = nc.vector.tensor_scalar(dst[:, t, :], src[:, t, :], moments[:, which, t, 0:1],
                                                   rstd[:, which, t:t + 1], ALU.subtract, ALU.mult)
                last.then_inc(ready, 1)

            def split_latents(n, par):
                dve.wait_ge(cc_ready, done(n))
                both = ps_m[:, :].rearrange("p (w s) -> p w s", w=2)
                nc.vector.tensor_copy(latent[:, par, :, :], both).then_inc(latent_hi, 1)
                dve.wait_ge(latent_hi, done(n))
                low = latent[L:P, par, :, :]
                nc.vector.tensor_tensor(low, both[L:P, :, :], low.bitcast(F32), ALU.subtract)\
                    .then_inc(latent_split, 1)

            def integrate(b, par, k):
                if k == 0:
                    dve.wait_ge(ny_ready, done(b))
                dve.wait_ge(lif, done(b * LIF_OPS + k - 1))
                ny = neg_y[:, par, :]
                step, op = (k + 2) // 3, (k + 2) % 3
                m_old = ny if step == 1 else mem[:, (step - 1) % 2, :]
                if k == 0:
                    ins = nc.vector.tensor_scalar(spikes[:, 0, :], ny, -THRESHOLD, None, ALU.is_lt)
                elif k == LIF_OPS - 1:
                    dve.wait_ge(res_ready, done(b))
                    ins = nc.vector.scalar_tensor_tensor(acc[:, :], spikes[:, (NUM_STEPS - 1) % 2, :],
                                                         1.0 / NUM_STEPS, acc[:, :], ALU.mult, ALU.add)
                elif op == 0:
                    ins = nc.vector.scalar_tensor_tensor(mem_t[:, :], m_old, BETA, ny, ALU.mult, ALU.add)
                elif op == 1:
                    ins = nc.vector.scalar_tensor_tensor(mem[:, step % 2, :], m_old, -THRESHOLD, mem_t[:, :],
                                                         ALU.is_lt, ALU.add)
                else:
                    ins = nc.vector.scalar_tensor_tensor(spikes[:, step % 2, :], mem[:, step % 2, :], -THRESHOLD,
                                                         spikes[:, (step - 1) % 2, :], ALU.is_lt, ALU.add)
                ins.then_inc(lif, 1)

            def finish(b, par):
                dve.wait_ge(out_ready, done(b))
                dve.wait_ge(lif, done(b * LIF_OPS + LIF_OPS - 1))
                dve.wait_ge(stored[par], 16 * (batch_base["i"] + 1))
                nc.vector.tensor_tensor(out_sb[:, par, :, :].rearrange("p t d -> p (t d)"), ps_m[:, 0:TT * D],
                                        acc[:, :], ALU.add).then_inc(final_done, 1)

            def prologue():
                start_counters(dve, "dve")
                for par in range(2):
                    dve.sem_inc(stored[par], 16)
                for n in range(2):
                    for which in range(2):
                        moments_of(n, n, which)
                        normalise(n, n, which)
                        if n == 0 and which == 1:
                            dve.wait_ge(w_loaded, W_ALL)
                            nc.vector.tensor_copy(wup_hi[:, :, :], wup_raw[:, :, :]).then_inc(setup_dve, 1)
                            dve.wait_ge(setup_pe, 1)
                            nc.vector.tensor_copy(wvo_sb[:, 0:PAIRS // 2, :],
                                                  ps_u[:, :].rearrange("p (j d) -> p j d", d=D))
                            nc.vector.tensor_copy(wvo_sb[:, PAIRS // 2:PAIRS, :],
                                                  ps_q[:, :, :].rearrange("p a (j d) -> p (a j) d", d=D))
                            dve.wait_ge(setup_dve, 1)
                            nc.vector.tensor_tensor(wup_lo[:, :, :], wup_raw[:, :, :],
                                                    wup_hi[:, :, :].bitcast(F32), ALU.subtract)\
                                .then_inc(setup_dve, 1)
                            split_latents(0, 0)
                            rotate(0, 0, 0)
                            rotate(0, 0, 1)
                rotate(1, 1, 0)
                rotate(1, 1, 1)
                row_max(0, 0, 0)
                row_max(0, 0, 1)
                reciprocals(0, 0, 0)
                reciprocals(0, 0, 1)
                rotate(2, 2, 0)
                rotate(2, 2, 1)
                for h in range(2):
                    row_max(1, 1, h)
                    reciprocals(1, 1, h)

            LIF_AT = [(0, 3), (3, 4), (4, 7), (7, 10), (10, 11), (11, 12), (12, 14), (14, 14)]
            assert LIF_AT[-1][1] == LIF_OPS

            def body(i):
                for s in range(BODY):
                    g, b0, p = i * BODY + s, s // PAIRS, s % PAIRS
                    b = i * UNROLL + b0
                    copy_u(g, s)
                    if not beyond(g + 2, STEPS):
                        row_max(g + 2, s + 2, 0)
                    if not beyond(g + 3, STEPS):
                        rotate(g + 3, s + 3, 0)
                    if not beyond(g + 2, STEPS):
                        reciprocals(g + 2, s + 2, 0)
                    if p == 1 and not beyond(b + 1, B):
                        split_latents(b + 1, (b0 + 1) % 2)
                    if p == PAIRS - 1:
                        finish(b, b0)
                    if not beyond(g + 2, STEPS):
                        row_max(g + 2, s + 2, 1)
                    if not beyond(g + 3, STEPS):
                        rotate(g + 3, s + 3, 1)
                    for k in range(*LIF_AT[p]):
                        integrate(b, b0, k)
                    if not beyond(b + 2, B):
                        if p == 4:
                            moments_of(b + 2, b0, 0)
                        elif p == 5:
                            normalise(b + 2, b0, 0)
                            moments_of(b + 2, b0, 1)
                        elif p == 6:
                            normalise(b + 2, b0, 1)
                    if not beyond(g + 2, STEPS):
                        reciprocals(g + 2, s + 2, 1)

            batch_base = {"i": 0}

            def with_base(i):
                batch_base["i"] = i
                body(i)

            run(dve, prologue, with_base)

        @block.gpsimd
        def _(pool):
            def add_rotated(g, s):
                pool.wait_ge(k_rot, done(g))
                pool.wait_ge(s_ready[1], done(g - 2))
                nc.gpsimd.tensor_tensor(qk[:, s % 2, :, :], rotated[:, s % 2, :, 0, :], rotated[:, s % 2, :, 1, :],
                                        ALU.add).then_inc(rope_done, 1)

            def divide(g, s, h):
                pool.wait_ge(rden_ready[h], done(g))
                pool.sem_inc(pool_waited, 1)
                for t in range(TT):
                    last = nc.gpsimd.tensor_scalar(prob[:, s % 2, h, t, :], prob[:, s % 2, h, t, :],
                                                   rden[:, s % 2, h, t:t + 1], None, ALU.mult)
                last.then_inc(p_norm[h], 1)

            def inverse_std(n, which):
                ag, eps, rs = ((aggr1, eps1, rstd1), (aggr2, eps2, rstd2))[which]
                pool.wait_ge(ag, done(n))
                pool.wait_ge(rs, done(n - 1))
                pool.sem_inc(pool_waited, 1)
                nc.gpsimd.tensor_scalar(var_eps[:, which, :], moments[:, which, :, 1], LN_EPS, None, ALU.add)\
                    .then_inc(eps, 1)
                pool.wait_ge(eps, done(n))
                pool.wait_ge((xn_ready, z_ready)[which], done(n - 1))
                nc.gpsimd.tensor_tensor(rstd[:, which, :], var_eps[:, which, :], minus_half[:, :], ALU.pow)\
                    .then_inc(rs, 1)

            def residual(b, par):
                pool.wait_ge(final_done, done(b - 1))
                pool.wait_ge(xn_ready, done(b))
                nc.gpsimd.tensor_tensor(acc[:, :], x_sb[:, par, :, :].rearrange("p t d -> p (t d)"),
                                        xn_sb[:, par, :, :].rearrange("p t d -> p (t d)"), ALU.add)\
                    .then_inc(res_ready, 1)

            def square(n, half):
                pool.wait_ge(relu_done, done(2 * n + half))
                c = slice(2 * half, 2 * half + 2)
                nc.gpsimd.tensor_tensor(hidden[:, c, :], relu_sb[:, c, :], relu_sb[:, c, :], ALU.mult)\
                    .then_inc(sq_done, 1)

            def prologue():
                start_counters(pool, "pool")
                nc.gpsimd.memset(minus_half[:, :], -0.5).then_inc(setup_pool, 1)
                pool.wait_ge(setup_pool, 1)
                inverse_std(0, 0)
                inverse_std(0, 1)
                add_rotated(0, 0)
                square(0, 0)
                square(0, 1)
                inverse_std(1, 0)
                inverse_std(1, 1)
                add_rotated(1, 1)
                divide(0, 0, 0)
                divide(0, 0, 1)
                add_rotated(2, 2)
                divide(1, 1, 0)
                divide(1, 1, 1)

            def body(i):
                for s in range(BODY):
                    g, b0, p = i * BODY + s, s // PAIRS, s % PAIRS
                    b = i * UNROLL + b0
                    if p == 0:
                        residual(b, b0)
                    if not beyond(g + 2, STEPS):
                        divide(g + 2, s + 2, 0)
                    if not beyond(g + 3, STEPS):
                        add_rotated(g + 3, s + 3)
                    if not beyond(b + 2, B):
                        if p == 4:
                            inverse_std(b + 2, 0)
                        elif p == 5:
                            inverse_std(b + 2, 1)
                    if not beyond(b + 1, B) and p in (3, 4):
                        square(b + 1, p - 3)
                    if not beyond(g + 2, STEPS):
                        divide(g + 2, s + 2, 1)

            run(pool, prologue, body)


def rope_tables():
    base = 10000.0
    inv_freq = 1.0 / base ** (np.arange(0, DH, 2, dtype=np.float32) / DH)
    freqs = np.outer(np.arange(S, dtype=np.float32), inv_freq)
    cos = np.concatenate([np.cos(freqs), np.cos(freqs)], -1)[:, ::2]
    sin = np.concatenate([np.sin(freqs), np.sin(freqs)], -1)[:, ::2]
    d = np.arange(P) % DH
    sign = np.where(d % 2 == 0, -1.0, 1.0).astype(np.float32)[:, None]
    one = np.stack([cos[:, d // 2].T, sin[:, d // 2].T * sign], 1).astype(np.float32)
    scale = np.float32(1.0 / np.sqrt(DH))
    return np.ascontiguousarray(np.stack([one * scale, one], 1))


def kernel(**inputs):
    import concourse.bacc as _bacc
    from concourse.bass_utils import run_bass_kernel_spmd as _run

    a = {k.replace("L0_", ""): np.asarray(v) for k, v in inputs.items()}

    def swapped(w):
        return w.reshape(-1, 2, w.shape[1])[:, ::-1].reshape(w.shape)

    wq, wk = a["attn_w_up_q"], a["attn_w_up_k"]
    dq, dkv = a["attn_w_down_q"].T, a["attn_w_down_kv"].T
    arrays = {
        "x": a["attn_x"],
        "wup": np.stack([wq.T, swapped(wq).T, wk.T, swapped(wk).T], 1),
        "wdown2": np.stack([np.concatenate([dq, dq], 1), np.concatenate([dkv, dkv], 1)], 1),
        "wkv_t": dkv,
        "wv": a["attn_w_up_v"].reshape(PAIRS, P, L).transpose(1, 0, 2),
        "wo_t": a["attn_w_out"].T.reshape(PAIRS, P, D).transpose(1, 0, 2),
        "ln_cols": np.stack([a["attn_ln_scale"], a["attn_ln_bias"]], 1),
        "wfc_t": a["ffn_W_fc"].T,
        "wproj_t": a["ffn_W_proj"].T.reshape(FC, P, D).transpose(1, 0, 2),
        "rope": rope_tables(),
        "ident": np.eye(P, dtype=np.float32),
    }
    nc = _bacc.Bacc("TRN2", target_bir_lowering=False, num_devices=1)
    ins, args = {}, []
    for name, v in arrays.items():
        v = np.ascontiguousarray(v)
        ins[f"in_{name}"] = v
        args.append(nc.dram_tensor(f"in_{name}", v.shape, mybir.dt.from_np(v.dtype), kind="ExternalInput").ap())
    args.append(nc.dram_tensor("out", (B, S, D), F32, kind="ExternalOutput").ap())
    build(nc, *args)
    r = _run(nc, [ins], core_ids=[0])
    return r.results[0]["out"]
```

```python
from contextlib import ExitStack

import numpy as np

import concourse.bass as bass
from concourse import mybir

F32 = mybir.dt.float32
F32R = mybir.dt.float32r
ALU = mybir.AluOpType
ACT = mybir.ActivationFunctionType
AXIS_X = mybir.AxisListType.X

B, S, D = 32, 256, 128
H, DH, L = 16, 64, 64
F = 512
P = 128
TT = S // P
PAIRS = H // 2
STEPS = B * PAIRS
UNROLL = 2
BODY = UNROLL * PAIRS
FC = F // P
LN_EPS = 1e-5
BETA, THRESHOLD, NUM_STEPS = 0.9, 1.0, 5
LEAD = {"project": 6, "add": 5, "split": 4, "scores": 3, "divide": 2, "transpose": 1, "multiply": 0}
FIRST = -max(LEAD.values())
PB = 4
HEAD = PB


def done(n):
    return n + 1 + HEAD


def outside(n, end):
    return isinstance(n, int) and not 0 <= n < end


def build(nc, x, wup, wdown2, wkv_t, wv, wo_t, ln_cols, wfc_t, wproj_t, rope, ident, out):
    ctx = ExitStack()
    with ctx:
        def sb(name, shape, dt=F32):
            return ctx.enter_context(nc.sbuf_tensor(name, shape, dt))

        def pb(name, shape):
            return ctx.enter_context(nc.psum_tensor(name, shape, F32))

        def sem(name):
            return ctx.enter_context(nc.semaphore(name))

        wup_raw = sb("wup_raw", [P, 2, H * DH])
        wup_hi = sb("wup_hi", [P, 2, H * DH], F32R)
        wup_lo = sb("wup_lo", [P, 2, H * DH], F32R)
        wdown_sb = sb("wdown_sb", [P, 2, 2 * L])
        wkv_sb = sb("wkv_sb", [P, L])
        wv_sb = sb("wv_sb", [P, PAIRS, L])
        wo_sb = sb("wo_sb", [P, PAIRS, D])
        wvo_sb = sb("wvo_sb", [P, PAIRS, D])
        ln_sb = sb("ln_sb", [P, 2])
        wfc_sb = sb("wfc_sb", [P, F])
        wproj_sb = sb("wproj_sb", [P, FC, D])
        rope_sb = sb("rope_sb", [P, 2, 2, S])
        ident_sb = sb("ident_sb", [P, P])
        minus_half = sb("minus_half", [P, TT])
        x_sb = sb("x_sb", [P, 2, TT, D])
        xn_sb = sb("xn_sb", [P, 2, TT, D])
        z_sb = sb("z_sb", [P, TT, D])
        stats = sb("stats", [P, 2, TT, 6])
        moments = sb("moments", [P, 2, TT, 2])
        var_eps = sb("var_eps", [P, 2, TT])
        rstd = sb("rstd", [P, 2, TT])
        h_t = sb("h_t", [P, S])
        xn_t = sb("xn_t", [P, S])
        latent = sb("latent", [P, 2, 2, S], F32R)
        ckv = sb("ckv", [P, 2, TT, L])
        relu_sb = sb("relu_sb", [P, FC, S])
        hidden = sb("hidden", [P, FC, S])
        neg_y = sb("neg_y", [P, 2, TT * D])
        mem_t = sb("mem_t", [P, TT * D])
        mem = sb("mem", [P, 2, TT * D])
        spikes = sb("spikes", [P, 2, TT * D])
        acc = sb("acc", [P, TT * D])
        out_sb = sb("out_sb", [P, 2, TT, D])
        cos_sin = sb("cos_sin", [P, 2, 2, 2, S])
        sin_sw = sb("sin_sw", [P, 2, 2, S])
        qk = sb("qk", [P, 2, 2, S])
        qk_hi = sb("qk_hi", [P, 2, 2, S], F32R)
        qk_lo = sb("qk_lo", [P, 2, 2, S], F32R)
        neg_max = sb("neg_max", [P, PB, 2, TT])
        den = sb("den", [P, PB, 2, TT])
        rden = sb("rden", [P, PB, 2, TT])
        prob = sb("prob", [P, PB, 2, TT, S])
        prob_t = sb("prob_t", [P, 2, 2, TT, S])
        u_t = sb("u_t", [P, PAIRS, S])
        ps_qk = [pb(f"ps_qk{i}", [P, 2, S]) for i in range(2)]
        ps_s = [pb(f"ps_s{h}", [P, TT, S]) for h in range(2)]
        ps_t = [pb(f"ps_t{h}", [P, TT, S]) for h in range(2)]
        ps_u = pb("ps_u", [P, 512])
        ps_m = pb("ps_m", [P, 512])

        w_loaded = sem("w_loaded")
        x_loaded = [sem(f"x_loaded{i}") for i in range(2)]
        stored = [sem(f"stored{i}") for i in range(2)]
        setup_dve = sem("setup_dve")
        setup_pool = sem("setup_pool")
        setup_pe = sem("setup_pe")
        dve_waited, pool_waited = sem("dve_waited"), sem("pool_waited")
        up_ready = sem("up_ready")
        rot_ready = sem("rot_ready")
        swapped = [sem(f"swapped{i}") for i in range(2)]
        rope_done = sem("rope_done")
        hi_ready, lo_ready = sem("hi_ready"), sem("lo_ready")
        s_ready = [sem(f"s_ready{h}") for h in range(2)]
        max_ready = [sem(f"max_ready{h}") for h in range(2)]
        exp_done = [sem(f"exp_done{h}") for h in range(2)]
        rden_ready = [sem(f"rden_ready{h}") for h in range(2)]
        p_norm = [sem(f"p_norm{h}") for h in range(2)]
        t_ready = [sem(f"t_ready{h}") for h in range(2)]
        pt_ready = [sem(f"pt_ready{h}") for h in range(2)]
        u_ready = sem("u_ready")
        u_evac = sem("u_evac")
        stats1, aggr1 = sem("stats1"), sem("aggr1")
        eps1, rstd1 = sem("eps1"), sem("rstd1")
        xn_ready = sem("xn_ready")
        stats2, aggr2 = sem("stats2"), sem("aggr2")
        eps2, rstd2 = sem("eps2"), sem("rstd2")
        z_ready = sem("z_ready")
        tr_ready, tr_evac = sem("tr_ready"), sem("tr_evac")
        cc_ready = sem("cc_ready")
        latent_hi, latent_split = sem("latent_hi"), sem("latent_split")
        ckv_mm, ckv_ready = sem("ckv_mm"), sem("ckv_ready")
        fc_ready, relu_done, sq_done = sem("fc_ready"), sem("relu_done"), sem("sq_done")
        y_ready, ny_ready = sem("y_ready"), sem("ny_ready")
        res_ready = sem("res_ready")
        lif = sem("lif")
        out_ready, final_done = sem("out_ready"), sem("final_done")
        LIF_OPS = 3 * NUM_STEPS - 1

        by_engine = {
            "pe": [up_ready, *s_ready, *t_ready, u_ready, tr_ready, cc_ready, ckv_mm, fc_ready, y_ready,
                   out_ready],
            "dve": [rot_ready, *max_ready, *rden_ready, p_norm[0], stats1, aggr1, xn_ready, stats2, aggr2,
                    z_ready, latent_hi, latent_split, lif, final_done],
            "act": [hi_ready, *exp_done, p_norm[1], *pt_ready, u_evac, tr_evac, ckv_ready, relu_done, ny_ready],
            "pool": [rope_done, lo_ready, eps1, rstd1, eps2, rstd2, sq_done, res_ready],
        }

        def start_counters(eng, who):
            for s in by_engine[who]:
                eng.sem_inc(s, HEAD)

        loads = [
            (ln_sb[:, :], ln_cols), (ident_sb[:, :], ident),
            (wdown_sb[:, :, :], wdown2), (wkv_sb[:, :], wkv_t),
            (wup_raw[0:L, :, :], wup), (wup_raw[L:P, :, :], wup),
            (rope_sb[:, :, :, :], rope),
            (wv_sb[:, :, :], wv), (wo_sb[:, :, :], wo_t),
            (wfc_sb[:, :], wfc_t), (wproj_sb[:, :, :], wproj_t),
        ]
        W_ALL = 16 * len(loads)
        x_v = x.rearrange("b (t p) d -> b p t d", p=P)
        out_v = out.rearrange("b (t p) d -> b p t d", p=P)

        block = ctx.enter_context(nc.Block())

        def run(eng, prologue, step):
            prologue()
            for s in range(FIRST, 0):
                step(0, s)
            with eng.Fori(0, B // UNROLL - 1) as i:
                for s in range(BODY):
                    step(i, s)
            for s in range(BODY):
                step(B // UNROLL - 1, s)

        @block.sync
        def _(sp):
            def load_x(n, par):
                sp.dma_start(x_sb[:, par, :, :], x_v[n]).then_inc(x_loaded[par], 16)

            def exchange(g, s):
                par = s % 2
                sp.wait_ge(rot_ready, done(g))
                for odd in range(2):
                    sp.dma_start(sin_sw[1 - odd::2, par, :, :], cos_sin[odd::2, par, 1, :, :])\
                        .then_inc(swapped[par], 16)

            def prologue():
                load_x(0, 0)
                load_x(1, 1)
                for dst, src in loads:
                    sp.dma_start(dst, src).then_inc(w_loaded, 16)

            def step(i, s):
                g, b0, p = i * BODY + s, s // PAIRS, s % PAIRS
                b, ahead = i * UNROLL + b0, LEAD["project"]
                if not outside(g + ahead, STEPS):
                    exchange(g + ahead, s + ahead)
                if s < 0:
                    return
                if p == 0 and not outside(b + 2, B):
                    sp.wait_ge(res_ready, done(b))
                    load_x(b + 2, b0)
                if p == PAIRS - 1:
                    sp.wait_ge(final_done, done(b))
                    sp.dma_start(out_v[b], out_sb[:, b0, :, :]).then_inc(stored[b0], 16)

            run(sp, prologue, step)
            for par in range(2):
                sp.wait_ge(stored[par], 16 * (B // 2) + 16)

        @block.tensor
        def _(pe):
            def project(g, s, i):
                if s % PAIRS == 0:
                    pe.wait_ge(latent_split, done(i * UNROLL + s // PAIRS))
                pe.wait_ge(rot_ready, done(g - 2))
                cols = slice((s % PAIRS) * P, (s % PAIRS + 1) * P)
                for which in range(2):
                    bank, rhs = ps_qk[s % 2][:, which, :], latent[:, (s // PAIRS) % 2, which, :]
                    nc.tensor.matmul(bank, wup_hi[:, which, cols], rhs, start=True, stop=False)
                    last = nc.tensor.matmul(bank, wup_lo[:, which, cols], rhs, start=False, stop=True)
                last.then_inc(up_ready, 1)

            def scores(g, s, h):
                if h == 0:
                    pe.wait_ge(lo_ready, done(g))
                pe.wait_ge(exp_done[h], done(g - 1))
                rows, par = slice(h * DH, (h + 1) * DH), s % 2
                parts = ((qk_lo, qk_hi), (qk_hi, qk_lo), (qk_hi, qk_hi))
                for t in range(TT):
                    for n, (q, k) in enumerate(parts):
                        last = nc.tensor.matmul(ps_s[h][:, t, :], q[rows, par, 0, t * P:(t + 1) * P],
                                                k[rows, par, 1, :], start=(n == 0), stop=(n == len(parts) - 1))
                last.then_inc(s_ready[h], 1)

            def transpose_probs(g, s, h):
                pe.wait_ge(p_norm[h], done(g))
                pe.wait_ge(pt_ready[h], done(g - 1))
                for kt in range(TT):
                    for t in range(TT):
                        last = nc.tensor.transpose(ps_t[h][:, kt, t * P:(t + 1) * P],
                                                   prob[:, s % PB, h, t, kt * P:(kt + 1) * P], ident_sb[:, :])
                last.then_inc(t_ready[h], 1)

            def weigh_latents(g, s, i):
                for h in range(2):
                    pe.wait_ge(pt_ready[h], done(g))
                pe.wait_ge(u_evac, done(g - 1))
                if s % PAIRS == 0:
                    pe.wait_ge(ckv_ready, done(i * UNROLL + s // PAIRS))
                for kt in range(TT):
                    for h in range(2):
                        last = nc.tensor.matmul(ps_u[h * L:(h + 1) * L, 0:S], ckv[:, (s // PAIRS) % 2, kt, :],
                                                prob_t[:, s % 2, h, kt, :], start=(kt == 0), stop=(kt == TT - 1))
                last.then_inc(u_ready, 1)

            def transpose_inputs(n, par):
                pe.wait_ge(z_ready, done(n))
                pe.wait_ge(final_done, done(n - 2))
                for src, at in ((z_sb[:, :, :], 0), (xn_sb[:, par, :, :], S)):
                    for t in range(TT):
                        last = nc.tensor.transpose(ps_m[:, at + t * P:at + (t + 1) * P], src[:, t, :], ident_sb[:, :])
                last.then_inc(tr_ready, 1)

            def latents(n):
                pe.wait_ge(tr_evac, done(n))
                for which in range(2):
                    last = nc.tensor.matmul(ps_m[:, which * S:(which + 1) * S], wdown_sb[:, which, :], h_t[:, :],
                                            start=True, stop=True)
                last.then_inc(cc_ready, 1)

            def latents_by_token(n):
                pe.wait_ge(latent_split, done(n))
                for t in range(TT):
                    last = nc.tensor.matmul(ps_m[:, t * L:(t + 1) * L], h_t[:, t * P:(t + 1) * P], wkv_sb[:, :],
                                            start=True, stop=True)
                last.then_inc(ckv_mm, 1)

            def ffn_in(n, half):
                if half == 0:
                    pe.wait_ge(ckv_ready, done(n))
                else:
                    pe.wait_ge(relu_done, done(2 * n))
                for j in range(2):
                    c = 2 * half + j
                    last = nc.tensor.matmul(ps_m[:, j * S:(j + 1) * S], wfc_sb[:, c * P:(c + 1) * P], xn_t[:, :],
                                            start=True, stop=True)
                last.then_inc(fc_ready, 1)

            def ffn_out(n):
                pe.wait_ge(sq_done, done(2 * n + 1))
                for t in range(TT):
                    for c in range(FC):
                        last = nc.tensor.matmul(ps_m[:, t * D:(t + 1) * D], hidden[:, c, t * P:(t + 1) * P],
                                                wproj_sb[:, c, :], start=(c == 0), stop=(c == FC - 1))
                last.then_inc(y_ready, 1)

            def attention_out(b, g):
                pe.wait_ge(u_evac, done(g))
                if not outside(b + 1, B):
                    pe.wait_ge(ny_ready, done(b + 1))
                for t in range(TT):
                    for pair in range(PAIRS):
                        last = nc.tensor.matmul(ps_m[:, t * D:(t + 1) * D], u_t[:, pair, t * P:(t + 1) * P],
                                                wvo_sb[:, pair, :], start=(pair == 0), stop=(pair == PAIRS - 1))
                last.then_inc(out_ready, 1)

            def extras(b, g, b0, p):
                n, par = b + 1, (b0 + 1) % 2
                if p == PAIRS - 1:
                    attention_out(b, g)
                if outside(n, B):
                    return
                if p == 0:
                    transpose_inputs(n, par)
                elif p == 1:
                    latents(n)
                elif p == 2:
                    latents_by_token(n)
                elif p in (3, 4):
                    ffn_in(n, p - 3)
                elif p == 6:
                    ffn_out(n)

            def prologue():
                start_counters(pe, "pe")
                pe.wait_ge(w_loaded, W_ALL)
                for half in range(2):
                    for j in range(PAIRS // 2):
                        pair = half * PAIRS // 2 + j
                        for h in range(2):
                            rows = slice(h * DH, (h + 1) * DH)
                            last = nc.tensor.matmul((ps_u, ps_m)[half][h * L:(h + 1) * L, j * D:(j + 1) * D],
                                                    wv_sb[rows, pair, :], wo_sb[rows, pair, :],
                                                    start=True, stop=True)
                last.then_inc(setup_pe, 1)
                pe.wait_ge(setup_dve, 3)
                transpose_inputs(0, 0)
                latents(0)
                latents_by_token(0)
                ffn_in(0, 0)
                ffn_in(0, 1)
                ffn_out(0)

            def step(i, s):
                g, b0, p = i * BODY + s, s // PAIRS, s % PAIRS
                if s >= 0:
                    weigh_latents(g, s, i)
                for h in range(2):
                    if not outside(g + LEAD["transpose"], STEPS):
                        transpose_probs(g + LEAD["transpose"], s + LEAD["transpose"], h)
                    if not outside(g + LEAD["scores"], STEPS):
                        scores(g + LEAD["scores"], s + LEAD["scores"], h)
                    if h == 0 and not outside(g + LEAD["project"], STEPS):
                        project(g + LEAD["project"], s + LEAD["project"], i)
                if s >= 0:
                    extras(i * UNROLL + b0, g, b0, p)

            run(pe, prologue, step)

        @block.scalar
        def _(act):
            def exponentials(g, s, h):
                act.wait_ge(max_ready[h], done(g))
                act.wait_ge(t_ready[h], done(g - PB))
                for t in range(TT):
                    last = nc.scalar.activation(prob[:, s % PB, h, t, :], ps_s[h][:, t, :], ACT.Exp,
                                                bias=neg_max[:, s % PB, h, t:t + 1],
                                                accum_out=den[:, s % PB, h, t:t + 1])
                last.then_inc(exp_done[h], 1)

            def copy_transposed(g, s, h):
                act.wait_ge(t_ready[h], done(g))
                act.wait_ge(u_ready, done(g - 2))
                nc.scalar.copy(prob_t[:, s % 2, h, :, :], ps_t[h][:, :, :]).then_inc(pt_ready[h], 1)

            def leading(g, s):
                act.wait_ge(rope_done, done(g))
                act.wait_ge(s_ready[1], done(g - 2))
                nc.scalar.copy(qk_hi[:, s % 2, :, :], qk[:, s % 2, :, :]).then_inc(hi_ready, 1)

            def divide_b(g, s):
                act.wait_ge(rden_ready[1], done(g))
                for t in range(TT):
                    last = nc.scalar.activation(prob[:, s % PB, 1, t, :], prob[:, s % PB, 1, t, :], ACT.Copy,
                                                scale=rden[:, s % PB, 1, t:t + 1])
                last.then_inc(p_norm[1], 1)

            def copy_u(g, s, i):
                act.wait_ge(u_ready, done(g))
                if s % PAIRS == 0:
                    act.wait_ge(out_ready, done(i * UNROLL + s // PAIRS - 1))
                nc.scalar.copy(u_t[:, s % PAIRS, :], ps_u[:, 0:S]).then_inc(u_evac, 1)

            def copy_inputs(n):
                act.wait_ge(tr_ready, done(n))
                act.wait_ge(w_loaded, W_ALL)
                nc.scalar.activation(h_t[:, :], ps_m[:, 0:S], ACT.Identity, bias=ln_sb[:, 1:2], scale=ln_sb[:, 0:1])
                nc.scalar.copy(xn_t[:, :], ps_m[:, S:2 * S]).then_inc(tr_evac, 1)

            def copy_latents(n, par):
                act.wait_ge(ckv_mm, done(n))
                nc.scalar.copy(ckv[:, par, :, :], ps_m[:, 0:TT * L].rearrange("p (t l) -> p t l", t=TT))\
                    .then_inc(ckv_ready, 1)

            def relu(n, half):
                act.wait_ge(fc_ready, done(2 * n + half))
                nc.scalar.activation(relu_sb[:, 2 * half:2 * half + 2, :],
                                     ps_m[:, :].rearrange("p (c s) -> p c s", c=2), ACT.Relu).then_inc(relu_done, 1)

            def negate_y(n, par):
                act.wait_ge(y_ready, done(n))
                nc.scalar.mul(neg_y[:, par, :], ps_m[:, 0:TT * D], -1.0).then_inc(ny_ready, 1)

            def prologue():
                start_counters(act, "act")
                copy_inputs(0)
                copy_latents(0, 0)
                relu(0, 0)
                relu(0, 1)
                negate_y(0, 0)

            def step(i, s):
                g, b0, p = i * BODY + s, s // PAIRS, s % PAIRS
                n, par = i * UNROLL + b0 + 1, (b0 + 1) % 2
                if not outside(g + LEAD["split"], STEPS):
                    leading(g + LEAD["split"], s + LEAD["split"])
                for h in range(2):
                    if not outside(g + LEAD["transpose"], STEPS):
                        copy_transposed(g + LEAD["transpose"], s + LEAD["transpose"], h)
                    if h == 0 and not outside(g + LEAD["divide"], STEPS):
                        divide_b(g + LEAD["divide"], s + LEAD["divide"])
                    if not outside(g + LEAD["scores"], STEPS):
                        exponentials(g + LEAD["scores"], s + LEAD["scores"], h)
                    if h == 0 and s >= 0:
                        copy_u(g, s, i)
                if s >= 0 and not outside(n, B):
                    if p == 0:
                        copy_inputs(n)
                    elif p == 2:
                        copy_latents(n, par)
                    elif p in (3, 4):
                        relu(n, p - 3)
                    elif p == 6:
                        negate_y(n, par)

            run(act, prologue, step)

        @block.vector
        def _(dve):
            def rotate(g, s):
                dve.wait_ge(up_ready, done(g))
                dve.wait_ge(rope_done, done(g - 2))
                for which in range(2):
                    last = nc.vector.tensor_tensor(
                        cos_sin[:, s % 2, :, which, :],
                        ps_qk[s % 2][:, which, :].unsqueeze(1).to_broadcast([P, 2, S]),
                        rope_sb[:, which, :, :], ALU.mult)
                last.then_inc(rot_ready, 1)

            def row_max(g, s, h):
                dve.wait_ge(s_ready[h], done(g))
                dve.wait_ge(exp_done[h], done(g - PB))
                nc.vector.tensor_reduce(neg_max[:, s % PB, h, :], ps_s[h][:, :, :], AXIS_X, ALU.max,
                                        negate=True).then_inc(max_ready[h], 1)

            def reciprocals(g, s, h):
                dve.wait_ge(exp_done[h], done(g))
                dve.wait_ge(p_norm[h], done(g - PB))
                nc.vector.reciprocal(rden[:, s % PB, h, :], den[:, s % PB, h, :]).then_inc(rden_ready[h], 1)

            def divide_a(g, s):
                dve.wait_ge(rden_ready[0], done(g))
                for t in range(TT):
                    last = nc.vector.tensor_scalar(prob[:, s % PB, 0, t, :], prob[:, s % PB, 0, t, :],
                                                   rden[:, s % PB, 0, t:t + 1], None, ALU.mult)
                last.then_inc(p_norm[0], 1)

            def moments_of(n, par, which, i):
                src, st, ag = ((x_sb, stats1, aggr1), (xn_sb, stats2, aggr2))[which]
                if which == 0:
                    dve.wait_ge(x_loaded[par], 16 * (i + 1))
                    dve.wait_ge(aggr1, done(n - 1))
                else:
                    dve.wait_ge(xn_ready, done(n))
                    dve.wait_ge(aggr2, done(n - 1))
                for t in range(TT):
                    last = nc.vector.bn_stats(stats[:, which, t, :], src[:, par, t, :])
                last.then_inc(st, 1)
                dve.wait_ge(st, done(n))
                dve.wait_ge((xn_ready, z_ready)[which], done(n - 1))
                dve.sem_inc(dve_waited, 1)
                for t in range(TT):
                    last = nc.vector.bn_aggr(moments[:, which, t, :], stats[:, which, t, :])
                last.then_inc(ag, 1)

            def normalise(n, par, which):
                if which == 0:
                    dve.wait_ge(rstd1, done(n))
                    dve.wait_ge(res_ready, done(n - 2))
                    dve.wait_ge(tr_ready, done(n - 2))
                    src, dst, ready = x_sb[:, par, :, :], xn_sb[:, par, :, :], xn_ready
                else:
                    dve.wait_ge(rstd2, done(n))
                    dve.wait_ge(tr_ready, done(n - 1))
                    src, dst, ready = xn_sb[:, par, :, :], z_sb[:, :, :], z_ready
                for t in range(TT):
                    last = nc.vector.tensor_scalar(dst[:, t, :], src[:, t, :], moments[:, which, t, 0:1],
                                                   rstd[:, which, t:t + 1], ALU.subtract, ALU.mult)
                last.then_inc(ready, 1)

            def split_latents(n, par):
                dve.wait_ge(cc_ready, done(n))
                both = ps_m[:, :].rearrange("p (w s) -> p w s", w=2)
                nc.vector.tensor_copy(latent[:, par, :, :], both).then_inc(latent_hi, 1)
                dve.wait_ge(latent_hi, done(n))
                low = latent[L:P, par, :, :]
                nc.vector.tensor_tensor(low, both[L:P, :, :], low.bitcast(F32), ALU.subtract)\
                    .then_inc(latent_split, 1)

            def integrate(b, par, k):
                if k == 0:
                    dve.wait_ge(ny_ready, done(b))
                dve.wait_ge(lif, done(b * LIF_OPS + k - 1))
                ny = neg_y[:, par, :]
                step, op = (k + 2) // 3, (k + 2) % 3
                m_old = ny if step == 1 else mem[:, (step - 1) % 2, :]
                if k == 0:
                    ins = nc.vector.tensor_scalar(spikes[:, 0, :], ny, -THRESHOLD, None, ALU.is_lt)
                elif k == LIF_OPS - 1:
                    dve.wait_ge(res_ready, done(b))
                    ins = nc.vector.scalar_tensor_tensor(acc[:, :], spikes[:, (NUM_STEPS - 1) % 2, :],
                                                         1.0 / NUM_STEPS, acc[:, :], ALU.mult, ALU.add)
                elif op == 0:
                    ins = nc.vector.scalar_tensor_tensor(mem_t[:, :], m_old, BETA, ny, ALU.mult, ALU.add)
                elif op == 1:
                    ins = nc.vector.scalar_tensor_tensor(mem[:, step % 2, :], m_old, -THRESHOLD, mem_t[:, :],
                                                         ALU.is_lt, ALU.add)
                else:
                    ins = nc.vector.scalar_tensor_tensor(spikes[:, step % 2, :], mem[:, step % 2, :], -THRESHOLD,
                                                         spikes[:, (step - 1) % 2, :], ALU.is_lt, ALU.add)
                ins.then_inc(lif, 1)

            def finish(b, par, i):
                dve.wait_ge(out_ready, done(b))
                dve.wait_ge(lif, done(b * LIF_OPS + LIF_OPS - 1))
                dve.wait_ge(stored[par], 16 * (i + 1))
                nc.vector.tensor_tensor(out_sb[:, par, :, :].rearrange("p t d -> p (t d)"), ps_m[:, 0:TT * D],
                                        acc[:, :], ALU.add).then_inc(final_done, 1)

            def prologue():
                start_counters(dve, "dve")
                for par in range(2):
                    dve.sem_inc(stored[par], 16)
                for n in range(2):
                    for which in range(2):
                        moments_of(n, n, which, 0)
                        normalise(n, n, which)
                        if n == 0 and which == 1:
                            dve.wait_ge(w_loaded, W_ALL)
                            nc.vector.tensor_copy(wup_hi[:, :, :], wup_raw[:, :, :]).then_inc(setup_dve, 1)
                            dve.wait_ge(setup_pe, 1)
                            nc.vector.tensor_copy(wvo_sb[:, 0:PAIRS // 2, :],
                                                  ps_u[:, :].rearrange("p (j d) -> p j d", d=D))
                            nc.vector.tensor_copy(wvo_sb[:, PAIRS // 2:PAIRS, :],
                                                  ps_m[:, :].rearrange("p (j d) -> p j d", d=D)).then_inc(setup_dve, 1)
                            dve.wait_ge(setup_dve, 2)
                            nc.vector.tensor_tensor(wup_lo[:, :, :], wup_raw[:, :, :],
                                                    wup_hi[:, :, :].bitcast(F32), ALU.subtract)\
                                .then_inc(setup_dve, 1)
                            split_latents(0, 0)

            LIF_AT = [(0, 3), (3, 4), (4, 7), (7, 10), (10, 11), (11, 12), (12, 14), (14, 14)]
            assert LIF_AT[-1][1] == LIF_OPS

            def step(i, s):
                g, b0, p = i * BODY + s, s // PAIRS, s % PAIRS
                b = i * UNROLL + b0
                if not outside(g + LEAD["divide"], STEPS):
                    for h in range(2):
                        reciprocals(g + LEAD["divide"], s + LEAD["divide"], h)
                    divide_a(g + LEAD["divide"], s + LEAD["divide"])
                if not outside(g + LEAD["scores"], STEPS):
                    row_max(g + LEAD["scores"], s + LEAD["scores"], 0)
                if not outside(g + LEAD["project"], STEPS):
                    rotate(g + LEAD["project"], s + LEAD["project"])
                if not outside(g + LEAD["scores"], STEPS):
                    row_max(g + LEAD["scores"], s + LEAD["scores"], 1)
                if s < 0:
                    return
                for k in range(*LIF_AT[p]):
                    integrate(b, b0, k)
                if p == 1 and not outside(b + 1, B):
                    split_latents(b + 1, (b0 + 1) % 2)
                if p == PAIRS - 1:
                    finish(b, b0, i)
                if not outside(b + 2, B):
                    if p == 4:
                        moments_of(b + 2, b0, 0, i + 1)
                    elif p == 5:
                        normalise(b + 2, b0, 0)
                        moments_of(b + 2, b0, 1, i + 1)
                    elif p == 6:
                        normalise(b + 2, b0, 1)

            run(dve, prologue, step)

        @block.gpsimd
        def _(pool):
            def add_rotated(g, s, i):
                pool.wait_ge(swapped[s % 2], (i * (BODY // 2) + s // 2 + 1) * 32)
                pool.wait_ge(lo_ready, done(g - 2))
                nc.gpsimd.tensor_tensor(qk[:, s % 2, :, :], cos_sin[:, s % 2, 0, :, :], sin_sw[:, s % 2, :, :],
                                        ALU.add).then_inc(rope_done, 1)

            def rest(g, s):
                pool.wait_ge(hi_ready, done(g))
                pool.wait_ge(s_ready[1], done(g - 2))
                nc.gpsimd.tensor_tensor(qk_lo[:, s % 2, :, :], qk[:, s % 2, :, :],
                                        qk_hi[:, s % 2, :, :].bitcast(F32), ALU.subtract).then_inc(lo_ready, 1)

            def inverse_std(n, which):
                ag, eps, rs = ((aggr1, eps1, rstd1), (aggr2, eps2, rstd2))[which]
                pool.wait_ge(ag, done(n))
                pool.wait_ge(rs, done(n - 1))
                pool.sem_inc(pool_waited, 1)
                nc.gpsimd.tensor_scalar(var_eps[:, which, :], moments[:, which, :, 1], LN_EPS, None, ALU.add)\
                    .then_inc(eps, 1)
                pool.wait_ge(eps, done(n))
                pool.wait_ge((xn_ready, z_ready)[which], done(n - 1))
                nc.gpsimd.tensor_tensor(rstd[:, which, :], var_eps[:, which, :], minus_half[:, :], ALU.pow)\
                    .then_inc(rs, 1)

            def residual(b, par):
                pool.wait_ge(final_done, done(b - 1))
                pool.wait_ge(xn_ready, done(b))
                nc.gpsimd.tensor_tensor(acc[:, :], x_sb[:, par, :, :].rearrange("p t d -> p (t d)"),
                                        xn_sb[:, par, :, :].rearrange("p t d -> p (t d)"), ALU.add)\
                    .then_inc(res_ready, 1)

            def square(n, half):
                pool.wait_ge(relu_done, done(2 * n + half))
                c = slice(2 * half, 2 * half + 2)
                nc.gpsimd.tensor_tensor(hidden[:, c, :], relu_sb[:, c, :], relu_sb[:, c, :], ALU.mult)\
                    .then_inc(sq_done, 1)

            def prologue():
                start_counters(pool, "pool")
                nc.gpsimd.memset(minus_half[:, :], -0.5).then_inc(setup_pool, 1)
                pool.wait_ge(setup_pool, 1)
                inverse_std(0, 0)
                inverse_std(0, 1)
                square(0, 0)
                square(0, 1)
                inverse_std(1, 0)
                inverse_std(1, 1)

            def step(i, s):
                g, b0, p = i * BODY + s, s // PAIRS, s % PAIRS
                b = i * UNROLL + b0
                if s >= 0 and p == 0:
                    residual(b, b0)
                if not outside(g + LEAD["split"], STEPS):
                    rest(g + LEAD["split"], s + LEAD["split"])
                if not outside(g + LEAD["add"], STEPS):
                    add_rotated(g + LEAD["add"], s + LEAD["add"], i)
                if s < 0:
                    return
                if not outside(b + 2, B):
                    if p == 4:
                        inverse_std(b + 2, 0)
                    elif p == 5:
                        inverse_std(b + 2, 1)
                if not outside(b + 1, B) and p in (3, 4):
                    square(b + 1, p - 3)

            run(pool, prologue, step)


def rope_tables():
    base = 10000.0
    inv_freq = 1.0 / base ** (np.arange(0, DH, 2, dtype=np.float32) / DH)
    freqs = np.outer(np.arange(S, dtype=np.float32), inv_freq)
    cos = np.concatenate([np.cos(freqs), np.cos(freqs)], -1)[:, ::2]
    sin = np.concatenate([np.sin(freqs), np.sin(freqs)], -1)[:, ::2]
    d = np.arange(P) % DH
    sign = np.where(d % 2 == 0, -1.0, 1.0).astype(np.float32)[:, None]
    one = np.stack([cos[:, d // 2].T, sin[:, d // 2].T * -sign], 1).astype(np.float32)
    scale = np.float32(1.0 / np.sqrt(DH))
    return np.ascontiguousarray(np.stack([one * scale, one], 1))


def kernel(**inputs):
    import concourse.bacc as _bacc
    from concourse.bass_utils import run_bass_kernel_spmd as _run

    a = {k.replace("L0_", ""): np.asarray(v) for k, v in inputs.items()}

    dq, dkv = a["attn_w_down_q"].T, a["attn_w_down_kv"].T
    arrays = {
        "x": a["attn_x"],
        "wup": np.stack([a["attn_w_up_q"].T, a["attn_w_up_k"].T], 1),
        "wdown2": np.stack([np.concatenate([dq, dq], 1), np.concatenate([dkv, dkv], 1)], 1),
        "wkv_t": dkv,
        "wv": a["attn_w_up_v"].reshape(PAIRS, P, L).transpose(1, 0, 2),
        "wo_t": a["attn_w_out"].T.reshape(PAIRS, P, D).transpose(1, 0, 2),
        "ln_cols": np.stack([a["attn_ln_scale"], a["attn_ln_bias"]], 1),
        "wfc_t": a["ffn_W_fc"].T,
        "wproj_t": a["ffn_W_proj"].T.reshape(FC, P, D).transpose(1, 0, 2),
        "rope": rope_tables(),
        "ident": np.eye(P, dtype=np.float32),
    }
    nc = _bacc.Bacc("TRN2", target_bir_lowering=False, num_devices=1)
    ins, args = {}, []
    for name, v in arrays.items():
        v = np.ascontiguousarray(v)
        ins[f"in_{name}"] = v
        args.append(nc.dram_tensor(f"in_{name}", v.shape, mybir.dt.from_np(v.dtype), kind="ExternalInput").ap())
    args.append(nc.dram_tensor("out", (B, S, D), F32, kind="ExternalOutput").ap())
    build(nc, *args)
    r = _run(nc, [ins], core_ids=[0])
    return r.results[0]["out"]
```

```python
from contextlib import ExitStack

import numpy as np

import concourse.bass as bass
from concourse import mybir

F32 = mybir.dt.float32
F32R = mybir.dt.float32r
ALU = mybir.AluOpType
ACT = mybir.ActivationFunctionType
AXIS_X = mybir.AxisListType.X

B, S, D = 32, 256, 128
H, DH, L = 16, 64, 64
F = 512
P = 128
TT = S // P
PAIRS = H // 2
STEPS = B * PAIRS
UNROLL = 2
BODY = UNROLL * PAIRS
FC = F // P
LN_EPS = 1e-5
BETA, THRESHOLD, NUM_STEPS = 0.9, 1.0, 5
LEAD = {"project": 6, "add": 5, "split": 4, "scores": 3, "scale": 2, "transpose": 1, "multiply": 0}
FIRST = -max(LEAD.values())
HEAD = 4


def done(n):
    return n + 1 + HEAD


def outside(n, end):
    return isinstance(n, int) and not 0 <= n < end


def spike_levels():
    f = np.float32

    def count(y):
        mem, fired, n = f(0), f(0), 0
        for _ in range(NUM_STEPS):
            mem = f(f(f(BETA) * mem) + y) - fired * f(THRESHOLD)
            fired = f(mem > f(THRESHOLD))
            n += int(fired)
        return n

    levels = []
    for k in range(NUM_STEPS):
        low, high = np.array([0.0, 4.0], f).view(np.int32)
        while high - low > 1:
            mid = np.int32((int(low) + int(high)) // 2)
            low, high = (mid, high) if count(mid.view(f)) <= k else (low, mid)
        levels.append(float(np.int32(low).view(f)))
    return levels


def build(nc, x, wup, wdown2, wkv_t, wv, wo_t, ln_cols, wfc_t, wproj_t, rope, ident, out):
    ctx = ExitStack()
    with ctx:
        def sb(name, shape, dt=F32):
            return ctx.enter_context(nc.sbuf_tensor(name, shape, dt))

        def pb(name, shape):
            return ctx.enter_context(nc.psum_tensor(name, shape, F32))

        def sem(name):
            return ctx.enter_context(nc.semaphore(name))

        wup_raw = sb("wup_raw", [P, 2, H * DH])
        wup_hi = sb("wup_hi", [P, 2, H * DH], F32R)
        wup_lo = sb("wup_lo", [P, 2, H * DH], F32R)
        wdown_sb = sb("wdown_sb", [P, 2, 2 * L])
        wkv_sb = sb("wkv_sb", [P, L])
        wv_sb = sb("wv_sb", [P, PAIRS, L])
        wo_sb = sb("wo_sb", [P, PAIRS, D])
        wvo_sb = sb("wvo_sb", [P, PAIRS, D])
        ln_sb = sb("ln_sb", [P, 2])
        wfc_sb = sb("wfc_sb", [P, F])
        wproj_sb = sb("wproj_sb", [P, FC, D])
        rope_sb = sb("rope_sb", [P, 2, 2, S])
        ident_sb = sb("ident_sb", [P, P])
        minus_half = sb("minus_half", [P, TT])
        x_sb = sb("x_sb", [P, 2, TT, D])
        xn_sb = sb("xn_sb", [P, 2, TT, D])
        z_sb = sb("z_sb", [P, TT, D])
        stats = sb("stats", [P, 2, TT, 6])
        moments = sb("moments", [P, 2, TT, 2])
        var_eps = sb("var_eps", [P, 2, TT])
        rstd = sb("rstd", [P, 2, TT])
        h_t = sb("h_t", [P, S])
        xn_t = sb("xn_t", [P, S])
        latent = sb("latent", [P, 2, 2, S], F32R)
        ckv = sb("ckv", [P, 2, TT, L])
        relu_sb = sb("relu_sb", [P, FC, S])
        hidden = sb("hidden", [P, FC, S])
        drive = sb("drive", [P, 2, TT * D])
        spikes = sb("spikes", [P, 2, TT * D])
        acc = sb("acc", [P, TT * D])
        out_sb = sb("out_sb", [P, 2, TT, D])
        cos_sin = sb("cos_sin", [P, 2, 2, 2, S])
        sin_sw = sb("sin_sw", [P, 2, 2, S])
        qk = sb("qk", [P, 2, 2, S])
        qk_hi = sb("qk_hi", [P, 2, 2, S], F32R)
        qk_lo = sb("qk_lo", [P, 2, 2, S], F32R)
        neg_max = sb("neg_max", [P, 2, 2, TT])
        den = sb("den", [P, 4, 2, TT])
        rden = sb("rden", [P, 2, 2, TT])
        prob = sb("prob", [P, 4, 2, TT, S])
        prob_t = sb("prob_t", [P, 2, 2, TT, S])
        u_t = sb("u_t", [P, PAIRS, S])
        ps_qk = [pb(f"ps_qk{i}", [P, 2, S]) for i in range(2)]
        ps_s = [pb(f"ps_s{h}", [P, TT, S]) for h in range(2)]
        ps_t = [pb(f"ps_t{h}", [P, TT, S]) for h in range(2)]
        ps_u = pb("ps_u", [P, 512])
        ps_m = pb("ps_m", [P, 512])

        levels = spike_levels()

        w_first, w_later = sem("w_first"), sem("w_later")
        x_loaded = [sem(f"x_loaded{i}") for i in range(2)]
        stored = [sem(f"stored{i}") for i in range(2)]
        setup_dve = sem("setup_dve")
        setup_pool = sem("setup_pool")
        setup_pe = sem("setup_pe")
        dve_waited, pool_waited = sem("dve_waited"), sem("pool_waited")
        up_ready = sem("up_ready")
        rot_ready = sem("rot_ready")
        swapped = [sem(f"swapped{i}") for i in range(2)]
        rope_done = sem("rope_done")
        hi_ready, lo_ready = sem("hi_ready"), sem("lo_ready")
        s_ready = [sem(f"s_ready{h}") for h in range(2)]
        max_ready = [sem(f"max_ready{h}") for h in range(2)]
        exp_done = [sem(f"exp_done{h}") for h in range(2)]
        rden_ready = sem("rden_ready")
        scaled = sem("scaled")
        t_ready = [sem(f"t_ready{h}") for h in range(2)]
        pt_ready = [sem(f"pt_ready{h}") for h in range(2)]
        u_ready = sem("u_ready")
        u_evac = sem("u_evac")
        stats1, aggr1 = sem("stats1"), sem("aggr1")
        eps1, rstd1 = sem("eps1"), sem("rstd1")
        xn_ready = sem("xn_ready")
        stats2, aggr2 = sem("stats2"), sem("aggr2")
        eps2, rstd2 = sem("eps2"), sem("rstd2")
        z_ready = sem("z_ready")
        tr_ready, tr_evac = sem("tr_ready"), sem("tr_evac")
        cc_ready = sem("cc_ready")
        latent_hi, latent_split = sem("latent_hi"), sem("latent_split")
        ckv_mm, ckv_ready = sem("ckv_mm"), sem("ckv_ready")
        fc_ready, relu_done, sq_done = sem("fc_ready"), sem("relu_done"), sem("sq_done")
        y_ready, drive_ready = sem("y_ready"), sem("drive_ready")
        res_ready = sem("res_ready")
        lif = sem("lif")
        out_ready, final_done = sem("out_ready"), sem("final_done")
        LIF_OPS = NUM_STEPS + 1

        by_engine = {
            "pe": [up_ready, *s_ready, *t_ready, u_ready, tr_ready, cc_ready, ckv_mm, fc_ready, y_ready,
                   out_ready],
            "dve": [rot_ready, *max_ready, rden_ready, scaled, stats1, aggr1, xn_ready, stats2, aggr2,
                    z_ready, latent_hi, latent_split, lif, final_done],
            "act": [u_evac, hi_ready, *exp_done, *pt_ready, tr_evac, ckv_ready, relu_done, drive_ready],
            "pool": [rope_done, lo_ready, eps1, rstd1, eps2, rstd2, sq_done, res_ready],
        }

        def start_counters(eng, who):
            for s in by_engine[who]:
                eng.sem_inc(s, HEAD)

        first_loads = [
            (ln_sb[:, :], ln_cols), (ident_sb[:, :], ident), (wdown_sb[:, :, :], wdown2),
            (wup_raw[0:L, :, :], wup), (wup_raw[L:P, :, :], wup), (wkv_sb[:, :], wkv_t),
            (rope_sb[:, :, :, :], rope),
        ]
        later_loads = [
            (wfc_sb[:, :], wfc_t), (wproj_sb[:, :, :], wproj_t), (wv_sb[:, :, :], wv), (wo_sb[:, :, :], wo_t),
        ]
        FIRST_LOADED, LATER_LOADED = 16 * len(first_loads), 16 * len(later_loads)
        x_v = x.rearrange("b (t p) d -> b p t d", p=P)
        out_v = out.rearrange("b (t p) d -> b p t d", p=P)

        block = ctx.enter_context(nc.Block())

        def run(eng, prologue, step):
            prologue()
            for s in range(BODY + FIRST, BODY):
                step(-1, s)
            for s in range(BODY):
                step(0, s)
            with eng.Fori(1, B // UNROLL - 1) as i:
                for s in range(BODY):
                    step(i, s)
            for s in range(BODY):
                step(B // UNROLL - 1, s)

        @block.sync
        def _(sp):
            def load_x(n, par):
                sp.dma_start(x_sb[:, par, :, :], x_v[n]).then_inc(x_loaded[par], 16)

            def store(b, par):
                sp.wait_ge(final_done, done(b))
                sp.dma_start(out_v[b], out_sb[:, par, :, :]).then_inc(stored[par], 16)

            def exchange(g, s):
                par = s % 2
                sp.wait_ge(rot_ready, done(g))
                for odd in range(2):
                    sp.dma_start(sin_sw[1 - odd::2, par, :, :], cos_sin[odd::2, par, 1, :, :])\
                        .then_inc(swapped[par], 16)

            def prologue():
                load_x(0, 0)
                for dst, src in first_loads:
                    sp.dma_start(dst, src).then_inc(w_first, 16)
                load_x(1, 1)
                for dst, src in later_loads:
                    sp.dma_start(dst, src).then_inc(w_later, 16)

            def step(i, s):
                g, b0, p = i * BODY + s, s // PAIRS, s % PAIRS
                b, ahead = i * UNROLL + b0, LEAD["project"]
                if not outside(g + ahead, STEPS):
                    exchange(g + ahead, s + ahead)
                if outside(b, B):
                    return
                if p == 1:
                    if not outside(b + 2, B):
                        sp.wait_ge(res_ready, done(b))
                        load_x(b + 2, b0)
                    if not outside(b - 1, B):
                        store(b - 1, 1 - b0)

            run(sp, prologue, step)
            store(B - 1, (B - 1) % 2)
            for par in range(2):
                sp.wait_ge(stored[par], 16 * (B // 2) + 16)

        @block.tensor
        def _(pe):
            def project(g, s, i):
                if s % PAIRS == 0:
                    pe.wait_ge(latent_split, done(i * UNROLL + s // PAIRS))
                pe.wait_ge(rot_ready, done(g - 2))
                cols = slice((s % PAIRS) * P, (s % PAIRS + 1) * P)
                for which in range(2):
                    bank, rhs = ps_qk[s % 2][:, which, :], latent[:, (s // PAIRS) % 2, which, :]
                    nc.tensor.matmul(bank, wup_hi[:, which, cols], rhs, start=True, stop=False)
                    last = nc.tensor.matmul(bank, wup_lo[:, which, cols], rhs, start=False, stop=True)
                last.then_inc(up_ready, 1)

            def scores(g, s, h):
                if h == 0:
                    pe.wait_ge(lo_ready, done(g))
                pe.wait_ge(exp_done[h], done(g - 1))
                rows, par = slice(h * DH, (h + 1) * DH), s % 2
                parts = ((qk_lo, qk_hi), (qk_hi, qk_lo), (qk_hi, qk_hi))
                for t in range(TT):
                    for n, (q, k) in enumerate(parts):
                        last = nc.tensor.matmul(ps_s[h][:, t, :], q[rows, par, 0, t * P:(t + 1) * P],
                                                k[rows, par, 1, :], start=(n == 0), stop=(n == len(parts) - 1))
                last.then_inc(s_ready[h], 1)

            def transpose_probs(g, s, h):
                pe.wait_ge(scaled, done(g))
                pe.wait_ge(pt_ready[h], done(g - 1))
                for kt in range(TT):
                    for t in range(TT):
                        last = nc.tensor.transpose(ps_t[h][:, kt, t * P:(t + 1) * P],
                                                   prob[:, s % 4, h, t, kt * P:(kt + 1) * P], ident_sb[:, :])
                last.then_inc(t_ready[h], 1)

            def weigh_latents(g, s, i):
                for h in range(2):
                    pe.wait_ge(pt_ready[h], done(g))
                pe.wait_ge(u_evac, done(g - 1))
                if s % PAIRS == 0:
                    pe.wait_ge(ckv_ready, done(i * UNROLL + s // PAIRS))
                for kt in range(TT):
                    for h in range(2):
                        last = nc.tensor.matmul(ps_u[h * L:(h + 1) * L, 0:S], ckv[:, (s // PAIRS) % 2, kt, :],
                                                prob_t[:, s % 2, h, kt, :], start=(kt == 0), stop=(kt == TT - 1))
                last.then_inc(u_ready, 1)

            def transpose_inputs(n, par):
                pe.wait_ge(z_ready, done(n))
                pe.wait_ge(drive_ready, done(n - 1))
                for src, at in ((z_sb[:, :, :], 0), (xn_sb[:, par, :, :], S)):
                    for t in range(TT):
                        last = nc.tensor.transpose(ps_m[:, at + t * P:at + (t + 1) * P], src[:, t, :], ident_sb[:, :])
                last.then_inc(tr_ready, 1)

            def latents(n):
                pe.wait_ge(tr_evac, done(n))
                for which in range(2):
                    last = nc.tensor.matmul(ps_m[:, which * S:(which + 1) * S], wdown_sb[:, which, :], h_t[:, :],
                                            start=True, stop=True)
                last.then_inc(cc_ready, 1)

            def latents_by_token(n):
                pe.wait_ge(latent_split, done(n))
                pe.wait_ge(final_done, done(n - 2))
                for t in range(TT):
                    last = nc.tensor.matmul(ps_m[:, t * L:(t + 1) * L], h_t[:, t * P:(t + 1) * P], wkv_sb[:, :],
                                            start=True, stop=True)
                last.then_inc(ckv_mm, 1)

            def ffn_in(n, half):
                if isinstance(n, int) and n == 0:
                    pe.wait_ge(w_later, LATER_LOADED)
                if half == 0:
                    pe.wait_ge(ckv_ready, done(n))
                else:
                    pe.wait_ge(relu_done, done(2 * n))
                for j in range(2):
                    c = 2 * half + j
                    last = nc.tensor.matmul(ps_m[:, j * S:(j + 1) * S], wfc_sb[:, c * P:(c + 1) * P], xn_t[:, :],
                                            start=True, stop=True)
                last.then_inc(fc_ready, 1)

            def ffn_out(n):
                if isinstance(n, int) and n == 0:
                    pe.wait_ge(setup_dve, 3)
                pe.wait_ge(sq_done, done(2 * n + 1))
                for t in range(TT):
                    for c in range(FC):
                        last = nc.tensor.matmul(ps_m[:, t * D:(t + 1) * D], hidden[:, c, t * P:(t + 1) * P],
                                                wproj_sb[:, c, :], start=(c == 0), stop=(c == FC - 1))
                last.then_inc(y_ready, 1)

            def attention_out(b, g):
                pe.wait_ge(u_evac, done(g))
                if not outside(b + 2, B):
                    pe.wait_ge(latent_split, done(b + 2))
                elif not outside(b + 1, B):
                    pe.wait_ge(drive_ready, done(b + 1))
                else:
                    pe.wait_ge(final_done, done(b - 1))
                for t in range(TT):
                    for pair in range(PAIRS):
                        last = nc.tensor.matmul(ps_m[:, t * D:(t + 1) * D], u_t[:, pair, t * P:(t + 1) * P],
                                                wvo_sb[:, pair, :], start=(pair == 0), stop=(pair == PAIRS - 1))
                last.then_inc(out_ready, 1)

            def value_by_output():
                pe.wait_ge(w_later, LATER_LOADED)
                pe.wait_ge(relu_done, done(1))
                for half in range(2):
                    for j in range(PAIRS // 2):
                        pair = half * PAIRS // 2 + j
                        for h in range(2):
                            rows = slice(h * DH, (h + 1) * DH)
                            last = nc.tensor.matmul((ps_u, ps_m)[half][h * L:(h + 1) * L, j * D:(j + 1) * D],
                                                    wv_sb[rows, pair, :], wo_sb[rows, pair, :],
                                                    start=True, stop=True)
                last.then_inc(setup_pe, 1)

            def extras(b, g, b0, p):
                n = b + 1
                if not outside(n, B):
                    if isinstance(b, int) and b == -1:
                        if p == 2:
                            latents_by_token(n)
                            ffn_in(n, 0)
                        elif p == 3:
                            ffn_in(n, 1)
                            value_by_output()
                    elif p == 0:
                        latents_by_token(n)
                    elif p in (1, 2):
                        ffn_in(n, p - 1)
                    if p == 4:
                        ffn_out(n)
                if not outside(b + 2, B):
                    if p == 5:
                        transpose_inputs(b + 2, b0)
                    elif p == 6:
                        latents(b + 2)
                if p == PAIRS - 1 and not outside(b, B):
                    attention_out(b, g)

            def prologue():
                start_counters(pe, "pe")
                pe.wait_ge(w_first, FIRST_LOADED)
                transpose_inputs(0, 0)
                latents(0)

            def step(i, s):
                g, b0, p = i * BODY + s, s // PAIRS, s % PAIRS
                if not outside(g + LEAD["transpose"], STEPS):
                    transpose_probs(g + LEAD["transpose"], s + LEAD["transpose"], 0)
                if not outside(g + LEAD["scores"], STEPS):
                    scores(g + LEAD["scores"], s + LEAD["scores"], 0)
                if not outside(g + LEAD["project"], STEPS):
                    project(g + LEAD["project"], s + LEAD["project"], i)
                if not outside(g, STEPS):
                    weigh_latents(g, s, i)
                if not outside(g + LEAD["transpose"], STEPS):
                    transpose_probs(g + LEAD["transpose"], s + LEAD["transpose"], 1)
                if not outside(g + LEAD["scores"], STEPS):
                    scores(g + LEAD["scores"], s + LEAD["scores"], 1)
                extras(i * UNROLL + b0, g, b0, p)

            run(pe, prologue, step)

        @block.scalar
        def _(act):
            def exponentials(g, s, h):
                act.wait_ge(max_ready[h], done(g))
                act.wait_ge(t_ready[h], done(g - 4))
                for t in range(TT):
                    last = nc.scalar.activation(prob[:, s % 4, h, t, :], ps_s[h][:, t, :], ACT.Exp,
                                                bias=neg_max[:, s % 2, h, t:t + 1],
                                                accum_out=den[:, s % 4, h, t:t + 1])
                last.then_inc(exp_done[h], 1)

            def leading(g, s):
                act.wait_ge(rope_done, done(g))
                act.wait_ge(s_ready[1], done(g - 2))
                nc.scalar.copy(qk_hi[:, s % 2, :, :], qk[:, s % 2, :, :]).then_inc(hi_ready, 1)

            def copy_transposed(g, s, h):
                act.wait_ge(t_ready[h], done(g))
                act.wait_ge(u_ready, done(g - 2))
                nc.scalar.copy(prob_t[:, s % 2, h, :, :], ps_t[h][:, :, :]).then_inc(pt_ready[h], 1)

            def copy_u(g, s, i):
                act.wait_ge(u_ready, done(g))
                if s % PAIRS == 0:
                    act.wait_ge(out_ready, done(i * UNROLL + s // PAIRS - 1))
                nc.scalar.copy(u_t[:, s % PAIRS, :], ps_u[:, 0:S]).then_inc(u_evac, 1)

            def copy_inputs(n):
                act.wait_ge(tr_ready, done(n))
                act.wait_ge(w_first, FIRST_LOADED)
                nc.scalar.activation(h_t[:, :], ps_m[:, 0:S], ACT.Identity, bias=ln_sb[:, 1:2], scale=ln_sb[:, 0:1])
                nc.scalar.copy(xn_t[:, :], ps_m[:, S:2 * S]).then_inc(tr_evac, 1)

            def copy_latents(n, par):
                act.wait_ge(ckv_mm, done(n))
                nc.scalar.copy(ckv[:, par, :, :], ps_m[:, 0:TT * L].rearrange("p (t l) -> p t l", t=TT))\
                    .then_inc(ckv_ready, 1)

            def relu(n, half):
                act.wait_ge(fc_ready, done(2 * n + half))
                nc.scalar.activation(relu_sb[:, 2 * half:2 * half + 2, :],
                                     ps_m[:, :].rearrange("p (c s) -> p c s", c=2), ACT.Relu).then_inc(relu_done, 1)

            def copy_y(n, par):
                act.wait_ge(y_ready, done(n))
                nc.scalar.copy(drive[:, par, :], ps_m[:, 0:TT * D]).then_inc(drive_ready, 1)

            def prologue():
                start_counters(act, "act")
                copy_inputs(0)

            def step(i, s):
                g, b0, p = i * BODY + s, s // PAIRS, s % PAIRS
                n, par = i * UNROLL + b0 + 1, (b0 + 1) % 2
                if not outside(g + LEAD["split"], STEPS):
                    leading(g + LEAD["split"], s + LEAD["split"])
                if p == PAIRS - 1 and not outside(g, STEPS):
                    copy_u(g, s, i)
                if not outside(g + LEAD["transpose"], STEPS):
                    copy_transposed(g + LEAD["transpose"], s + LEAD["transpose"], 0)
                if not outside(g + LEAD["scores"], STEPS):
                    exponentials(g + LEAD["scores"], s + LEAD["scores"], 0)
                if not outside(g + LEAD["transpose"], STEPS):
                    copy_transposed(g + LEAD["transpose"], s + LEAD["transpose"], 1)
                if p < PAIRS - 1 and not outside(g, STEPS):
                    copy_u(g, s, i)
                if not outside(g + LEAD["scores"], STEPS):
                    exponentials(g + LEAD["scores"], s + LEAD["scores"], 1)
                if not outside(n, B):
                    if isinstance(n, int) and n == 0:
                        if p == 2:
                            copy_latents(n, par)
                            relu(n, 0)
                        elif p == 3:
                            relu(n, 1)
                    elif p == 0:
                        copy_latents(n, par)
                    elif p in (1, 2):
                        relu(n, p - 1)
                    if p == 4:
                        copy_y(n, par)
                if p == 5 and not outside(n + 1, B):
                    copy_inputs(n + 1)

            run(act, prologue, step)

        @block.vector
        def _(dve):
            def rotate(g, s):
                dve.wait_ge(up_ready, done(g))
                dve.wait_ge(rope_done, done(g - 2))
                for which in range(2):
                    last = nc.vector.tensor_tensor(
                        cos_sin[:, s % 2, :, which, :],
                        ps_qk[s % 2][:, which, :].unsqueeze(1).to_broadcast([P, 2, S]),
                        rope_sb[:, which, :, :], ALU.mult)
                last.then_inc(rot_ready, 1)

            def row_max(g, s, h):
                dve.wait_ge(s_ready[h], done(g))
                dve.wait_ge(exp_done[h], done(g - 2))
                nc.vector.tensor_reduce(neg_max[:, s % 2, h, :], ps_s[h][:, :, :], AXIS_X, ALU.max,
                                        negate=True).then_inc(max_ready[h], 1)

            def scale(g, s):
                for h in range(2):
                    dve.wait_ge(exp_done[h], done(g))
                dve.wait_ge(scaled, done(g - 2))
                nc.vector.reciprocal(rden[:, s % 2, :, :], den[:, s % 4, :, :]).then_inc(rden_ready, 1)
                dve.wait_ge(rden_ready, done(g))
                for h in range(2):
                    for t in range(TT):
                        rows = prob[:, s % 4, h, t, :]
                        last = nc.vector.tensor_scalar(rows, rows, rden[:, s % 2, h, t:t + 1], None, ALU.mult)
                last.then_inc(scaled, 1)

            def moments_of(n, par, which, i):
                src, st, ag = ((x_sb, stats1, aggr1), (xn_sb, stats2, aggr2))[which]
                if which == 0:
                    dve.wait_ge(x_loaded[par], 16 * (i + 1))
                    dve.wait_ge(aggr1, done(n - 1))
                else:
                    dve.wait_ge(xn_ready, done(n))
                    dve.wait_ge(aggr2, done(n - 1))
                for t in range(TT):
                    last = nc.vector.bn_stats(stats[:, which, t, :], src[:, par, t, :])
                last.then_inc(st, 1)
                dve.wait_ge(st, done(n))
                dve.wait_ge((xn_ready, z_ready)[which], done(n - 1))
                dve.sem_inc(dve_waited, 1)
                for t in range(TT):
                    last = nc.vector.bn_aggr(moments[:, which, t, :], stats[:, which, t, :])
                last.then_inc(ag, 1)

            def normalise(n, par, which):
                if which == 0:
                    dve.wait_ge(rstd1, done(n))
                    dve.wait_ge(res_ready, done(n - 2))
                    dve.wait_ge(tr_ready, done(n - 2))
                    src, dst, ready = x_sb[:, par, :, :], xn_sb[:, par, :, :], xn_ready
                else:
                    dve.wait_ge(rstd2, done(n))
                    dve.wait_ge(tr_ready, done(n - 1))
                    src, dst, ready = xn_sb[:, par, :, :], z_sb[:, :, :], z_ready
                for t in range(TT):
                    last = nc.vector.tensor_scalar(dst[:, t, :], src[:, t, :], moments[:, which, t, 0:1],
                                                   rstd[:, which, t:t + 1], ALU.subtract, ALU.mult)
                last.then_inc(ready, 1)

            def split_latents(n, par):
                dve.wait_ge(cc_ready, done(n))
                both = ps_m[:, :].rearrange("p (w s) -> p w s", w=2)
                nc.vector.tensor_copy(latent[:, par, :, :], both).then_inc(latent_hi, 1)
                dve.wait_ge(latent_hi, done(n))
                low = latent[L:P, par, :, :]
                nc.vector.tensor_tensor(low, both[L:P, :, :], low.bitcast(F32), ALU.subtract)\
                    .then_inc(latent_split, 1)

            def integrate(b, par, k):
                if k == 0:
                    dve.wait_ge(drive_ready, done(b))
                dve.wait_ge(lif, done(b * LIF_OPS + k - 1))
                if k == 0:
                    ins = nc.vector.tensor_scalar(spikes[:, 0, :], drive[:, par, :], levels[0], None, ALU.is_gt)
                elif k < NUM_STEPS:
                    ins = nc.vector.scalar_tensor_tensor(spikes[:, k % 2, :], drive[:, par, :], levels[k],
                                                         spikes[:, (k - 1) % 2, :], ALU.is_gt, ALU.add)
                else:
                    dve.wait_ge(res_ready, done(b))
                    ins = nc.vector.scalar_tensor_tensor(acc[:, :], spikes[:, (NUM_STEPS - 1) % 2, :],
                                                         1.0 / NUM_STEPS, acc[:, :], ALU.mult, ALU.add)
                ins.then_inc(lif, 1)

            def finish(b, par, i):
                dve.wait_ge(out_ready, done(b))
                dve.wait_ge(lif, done(b * LIF_OPS + LIF_OPS - 1))
                dve.wait_ge(stored[par], 16 * (i + 1))
                nc.vector.tensor_tensor(out_sb[:, par, :, :].rearrange("p t d -> p (t d)"), ps_m[:, 0:TT * D],
                                        acc[:, :], ALU.add).then_inc(final_done, 1)

            def prologue():
                start_counters(dve, "dve")
                for par in range(2):
                    dve.sem_inc(stored[par], 16)
                for which in range(2):
                    moments_of(0, 0, which, 0)
                    normalise(0, 0, which)
                dve.wait_ge(w_first, FIRST_LOADED)
                nc.vector.tensor_copy(wup_hi[:, :, :], wup_raw[:, :, :]).then_inc(setup_dve, 1)
                dve.wait_ge(setup_dve, 1)
                nc.vector.tensor_tensor(wup_lo[:, :, :], wup_raw[:, :, :], wup_hi[:, :, :].bitcast(F32),
                                        ALU.subtract).then_inc(setup_dve, 1)
                split_latents(0, 0)

            def copy_value_by_output():
                dve.wait_ge(setup_pe, 1)
                nc.vector.tensor_copy(wvo_sb[:, 0:PAIRS // 2, :], ps_u[:, :].rearrange("p (j d) -> p j d", d=D))
                nc.vector.tensor_copy(wvo_sb[:, PAIRS // 2:PAIRS, :],
                                      ps_m[:, :].rearrange("p (j d) -> p j d", d=D)).then_inc(setup_dve, 1)

            LIF_AT = [(0, 0), (0, 1), (1, 1), (1, 1), (1, 1), (1, 3), (3, 5), (5, 6)]
            assert LIF_AT[-1][1] == LIF_OPS

            def step(i, s):
                g, b0, p = i * BODY + s, s // PAIRS, s % PAIRS
                b = i * UNROLL + b0
                if p == 0 and not outside(b - 1, B):
                    finish(b - 1, 1 - b0, i - 1 + b0)
                if p == PAIRS - 1 and not outside(b + 2, B):
                    split_latents(b + 2, b0)
                if not outside(g + LEAD["scores"], STEPS):
                    row_max(g + LEAD["scores"], s + LEAD["scores"], 0)
                if not outside(g + LEAD["scale"], STEPS):
                    scale(g + LEAD["scale"], s + LEAD["scale"])
                if not outside(g + LEAD["project"], STEPS):
                    rotate(g + LEAD["project"], s + LEAD["project"])
                if not outside(g + LEAD["scores"], STEPS):
                    row_max(g + LEAD["scores"], s + LEAD["scores"], 1)
                if not outside(b, B):
                    for k in range(*LIF_AT[p]):
                        integrate(b, b0, k)
                elif p == 3:
                    copy_value_by_output()
                if not outside(b + 2, B):
                    if p == 2:
                        moments_of(b + 2, b0, 0, i + 1)
                    elif p == 3:
                        normalise(b + 2, b0, 0)
                        moments_of(b + 2, b0, 1, i + 1)
                    elif p == 4:
                        normalise(b + 2, b0, 1)

            run(dve, prologue, step)
            finish(B - 1, (B - 1) % 2, B // UNROLL - 1)

        @block.gpsimd
        def _(pool):
            def add_rotated(g, s, i):
                pool.wait_ge(swapped[s % 2], (i * (BODY // 2) + s // 2 + 1) * 32)
                pool.wait_ge(lo_ready, done(g - 2))
                nc.gpsimd.tensor_tensor(qk[:, s % 2, :, :], cos_sin[:, s % 2, 0, :, :], sin_sw[:, s % 2, :, :],
                                        ALU.add).then_inc(rope_done, 1)

            def rest(g, s):
                pool.wait_ge(hi_ready, done(g))
                pool.wait_ge(s_ready[1], done(g - 2))
                nc.gpsimd.tensor_tensor(qk_lo[:, s % 2, :, :], qk[:, s % 2, :, :],
                                        qk_hi[:, s % 2, :, :].bitcast(F32), ALU.subtract).then_inc(lo_ready, 1)

            def inverse_std(n, which):
                ag, eps, rs = ((aggr1, eps1, rstd1), (aggr2, eps2, rstd2))[which]
                pool.wait_ge(ag, done(n))
                pool.wait_ge(rs, done(n - 1))
                pool.sem_inc(pool_waited, 1)
                nc.gpsimd.tensor_scalar(var_eps[:, which, :], moments[:, which, :, 1], LN_EPS, None, ALU.add)\
                    .then_inc(eps, 1)
                pool.wait_ge(eps, done(n))
                pool.wait_ge((xn_ready, z_ready)[which], done(n - 1))
                nc.gpsimd.tensor_tensor(rstd[:, which, :], var_eps[:, which, :], minus_half[:, :], ALU.pow)\
                    .then_inc(rs, 1)

            def residual(b, par):
                pool.wait_ge(final_done, done(b - 1))
                pool.wait_ge(xn_ready, done(b))
                nc.gpsimd.tensor_tensor(acc[:, :], x_sb[:, par, :, :].rearrange("p t d -> p (t d)"),
                                        xn_sb[:, par, :, :].rearrange("p t d -> p (t d)"), ALU.add)\
                    .then_inc(res_ready, 1)

            def square(n, half):
                pool.wait_ge(relu_done, done(2 * n + half))
                c = slice(2 * half, 2 * half + 2)
                nc.gpsimd.tensor_tensor(hidden[:, c, :], relu_sb[:, c, :], relu_sb[:, c, :], ALU.mult)\
                    .then_inc(sq_done, 1)

            def prologue():
                start_counters(pool, "pool")
                nc.gpsimd.memset(minus_half[:, :], -0.5).then_inc(setup_pool, 1)
                pool.wait_ge(setup_pool, 1)
                inverse_std(0, 0)
                inverse_std(0, 1)

            def step(i, s):
                g, b0, p = i * BODY + s, s // PAIRS, s % PAIRS
                b = i * UNROLL + b0
                if not outside(g + LEAD["split"], STEPS):
                    rest(g + LEAD["split"], s + LEAD["split"])
                if not outside(g + LEAD["add"], STEPS):
                    add_rotated(g + LEAD["add"], s + LEAD["add"], i)
                if p == 0 and not outside(b, B):
                    residual(b, b0)
                if not outside(b + 2, B):
                    if p == 3:
                        inverse_std(b + 2, 0)
                    elif p == 4:
                        inverse_std(b + 2, 1)
                if not outside(b + 1, B) and p in (2, 3):
                    square(b + 1, p - 2)

            run(pool, prologue, step)


def rope_tables():
    base = 10000.0
    inv_freq = 1.0 / base ** (np.arange(0, DH, 2, dtype=np.float32) / DH)
    freqs = np.outer(np.arange(S, dtype=np.float32), inv_freq)
    cos = np.concatenate([np.cos(freqs), np.cos(freqs)], -1)[:, ::2]
    sin = np.concatenate([np.sin(freqs), np.sin(freqs)], -1)[:, ::2]
    d = np.arange(P) % DH
    sign = np.where(d % 2 == 0, -1.0, 1.0).astype(np.float32)[:, None]
    one = np.stack([cos[:, d // 2].T, sin[:, d // 2].T * -sign], 1).astype(np.float32)
    scale = np.float32(1.0 / np.sqrt(DH))
    return np.ascontiguousarray(np.stack([one * scale, one], 1))


def kernel(**inputs):
    import concourse.bacc as _bacc
    from concourse.bass_utils import run_bass_kernel_spmd as _run

    a = {k.replace("L0_", ""): np.asarray(v) for k, v in inputs.items()}

    dq, dkv = a["attn_w_down_q"].T, a["attn_w_down_kv"].T
    arrays = {
        "x": a["attn_x"],
        "wup": np.stack([a["attn_w_up_q"].T, a["attn_w_up_k"].T], 1),
        "wdown2": np.stack([np.concatenate([dq, dq], 1), np.concatenate([dkv, dkv], 1)], 1),
        "wkv_t": dkv,
        "wv": a["attn_w_up_v"].reshape(PAIRS, P, L).transpose(1, 0, 2),
        "wo_t": a["attn_w_out"].T.reshape(PAIRS, P, D).transpose(1, 0, 2),
        "ln_cols": np.stack([a["attn_ln_scale"], a["attn_ln_bias"]], 1),
        "wfc_t": a["ffn_W_fc"].T,
        "wproj_t": a["ffn_W_proj"].T.reshape(FC, P, D).transpose(1, 0, 2),
        "rope": rope_tables(),
        "ident": np.eye(P, dtype=np.float32),
    }
    nc = _bacc.Bacc("TRN2", target_bir_lowering=False, num_devices=1)
    ins, args = {}, []
    for name, v in arrays.items():
        v = np.ascontiguousarray(v)
        ins[f"in_{name}"] = v
        args.append(nc.dram_tensor(f"in_{name}", v.shape, mybir.dt.from_np(v.dtype), kind="ExternalInput").ap())
    args.append(nc.dram_tensor("out", (B, S, D), F32, kind="ExternalOutput").ap())
    build(nc, *args)
    r = _run(nc, [ins], core_ids=[0])
    return r.results[0]["out"]
```
